# Optimizing a Trainium2 kernel written in Bass

```python
import numpy as np
import jax
import jax.numpy as jnp

def _softmax(x, axis=-1):
    return jax.nn.softmax(x, axis=axis)
def _gelu(x):
    return jax.nn.gelu(x, approximate=True)
def _silu(x):
    return jax.nn.silu(x)
def _sigmoid(x):
    return jax.nn.sigmoid(x)
def _layernorm(x, axis=-1, eps=1e-5):
    m = jnp.mean(x, axis=axis, keepdims=True)
    v = jnp.var(x, axis=axis, keepdims=True)
    return (x - m) / jnp.sqrt(v + eps)
def _scatter_add(tgt, idx, src, axis=0):
    return tgt.at[idx].add(src)
def _segment_sum(src, seg, n):
    return jax.ops.segment_sum(src, seg, n)

kernel_name = 'mk_conv_preact_d2_conv_nchw512_f38dea'

def setup_inputs(seed: int = 0):
    np.random.seed(seed)
    _w = jnp.asarray
    def _rec_inputs():
        import jax
        import jax.numpy as jnp
        _gk = jax.random.key(seed)
        x = -0.0002928 + 1 * jax.random.normal(jax.random.fold_in(_gk, 1), (8, 512, 32, 32), jnp.float32)
        return x
    x = _rec_inputs()
    def _L0_conv_setup():
        import jax, jax.numpy as jnp
        import numpy as np
        NUM_HEADS = 8
        key = jax.random.key(seed)
        ks = jax.random.split(key, 7)
        C = 512
        x = jax.random.normal(ks[0], (8, C, 32, 32), dtype=jnp.float32)
        s = 1.0 / np.sqrt(C)
        Wq = jax.random.normal(ks[1], (C, C), dtype=jnp.float32) * s
        bq = jax.random.normal(ks[2], (C,), dtype=jnp.float32) * 0.02
        Wk = jax.random.normal(ks[3], (C, C), dtype=jnp.float32) * s
        bk = jax.random.normal(ks[4], (C,), dtype=jnp.float32) * 0.02
        Wv = jax.random.normal(ks[5], (C, C), dtype=jnp.float32) * s
        bv = jax.random.normal(ks[6], (C,), dtype=jnp.float32) * 0.02
        return {'x': x, 'Wq': Wq, 'bq': bq, 'Wk': Wk, 'bk': bk, 'Wv': Wv, 'bv': bv}
    _L0_conv_all = _L0_conv_setup()
    _L0_conv_in = {k: v for k, v in _L0_conv_all.items() if k in ('Wq', 'bq', 'Wk', 'bk', 'Wv', 'bv', )}
    del _L0_conv_all

    def _L1_conv_setup():
        import jax, jax.numpy as jnp
        import numpy as np
        from jax import lax

        def _get_mu(x):
            bs, depth, h, w = x.shape
            ix = jnp.arange(1, h + 1, dtype=x.dtype).reshape(1, 1, h, 1)
            iy = jnp.arange(1, w + 1, dtype=x.dtype).reshape(1, 1, 1, w)
            sumX = jnp.maximum(x.sum((2, 3)), 1e-09)
            mu_x = jnp.maximum(jnp.round((ix * x).sum((2, 3)) / sumX), 1.0)
            mu_y = jnp.maximum(jnp.round((iy * x).sum((2, 3)) / sumX), 1.0)
            lin = jnp.linspace(-1.0, 1.0, h, dtype=x.dtype)
            mu_xg = lin[(mu_x - 1.0).astype(jnp.int32)]
            mu_yg = lin[(mu_y - 1.0).astype(jnp.int32)]
            return (mu_xg, mu_yg)

        def _get_mask(x, mask_weight, filt):
            bs, depth, h, w = x.shape
            mu_x, mu_y = _get_mu(x)
            posX = jnp.linspace(-1.0, 1.0, h, dtype=x.dtype).reshape(1, 1, h, 1)
            posY = jnp.linspace(-1.0, 1.0, w, dtype=x.dtype).reshape(1, 1, 1, w)
            m = jnp.abs(posX - mu_x[:, :, None, None]) + jnp.abs(posY - mu_y[:, :, None, None])
            m = 1.0 - m * mask_weight.reshape(1, depth, 1, 1)
            m = jnp.maximum(m, -1.0)
            m = jnp.where(filt.reshape(1, depth, 1, 1) == 1.0, m, 1.0)
            return m
        key = jax.random.key(seed)
        k1, k2, k3, k4 = jax.random.split(key, 4)
        bs, depth, h, w = (32, 512, 28, 28)
        out_c, kh, kw = (512, 3, 3)
        x = jax.random.uniform(k1, (bs, depth, h, w), dtype=jnp.float32)
        weight = jax.random.normal(k2, (out_c, depth, kh, kw), dtype=jnp.float32) * 0.02
        bias = jax.random.normal(k3, (out_c,), dtype=jnp.float32) * 0.02
        mask_weight = jax.random.uniform(k4, (depth,), dtype=jnp.float32)
        filt = jnp.ones((depth, 1), dtype=jnp.float32)
        return {'x': x, 'weight': weight, 'bias': bias, 'mask_weight': mask_weight, 'filter': filt, 'padding': 1}
    _L1_conv_all = _L1_conv_setup()
    _L1_conv_in = {k: v for k, v in _L1_conv_all.items() if k in ('weight', 'bias', 'mask_weight', 'filter', )}
    del _L1_conv_all

    return {
        "x": x,
        "L0_conv_Wq": _L0_conv_in["Wq"],
        "L0_conv_bq": _L0_conv_in["bq"],
        "L0_conv_Wk": _L0_conv_in["Wk"],
        "L0_conv_bk": _L0_conv_in["bk"],
        "L0_conv_Wv": _L0_conv_in["Wv"],
        "L0_conv_bv": _L0_conv_in["bv"],
        "L1_conv_weight": _L1_conv_in["weight"],
        "L1_conv_bias": _L1_conv_in["bias"],
        "L1_conv_mask_weight": _L1_conv_in["mask_weight"],
        "L1_conv_filter": _L1_conv_in["filter"],
    }

def reference(x, L0_conv_Wq, L0_conv_bq, L0_conv_Wk, L0_conv_bk, L0_conv_Wv, L0_conv_bv, L1_conv_weight, L1_conv_bias, L1_conv_mask_weight, L1_conv_filter):
    import jax
    import jax.numpy as jnp
    def _L0_conv_ref(x, Wq, bq, Wk, bk, Wv, bv):
        import jax, jax.numpy as jnp
        import numpy as np
        NUM_HEADS = 8
        B, C, W, H = x.shape
        hd = C // NUM_HEADS
        S = W * H
        t = x.reshape(B, C, S).transpose(0, 2, 1)
        q = t @ Wq.T + bq
        k = t @ Wk.T + bk
        v = t @ Wv.T + bv
        q = q.reshape(B * NUM_HEADS, S, hd)
        k = k.reshape(B * NUM_HEADS, S, hd)
        v = v.reshape(B * NUM_HEADS, S, hd)
        scores = jnp.einsum('gqd,gkd->gqk', q, k) / jnp.sqrt(jnp.asarray(hd, x.dtype))
        attn = jax.nn.softmax(scores, axis=-1)
        wv = jnp.einsum('gqk,gkd->gqd', attn, v)
        wv = wv.reshape(B, S, NUM_HEADS, hd).transpose(0, 2, 3, 1)
        return wv.reshape(B, C, W, H)

    def _L1_conv_ref(x, weight, bias, mask_weight, filter, padding):
        import jax, jax.numpy as jnp
        import numpy as np
        from jax import lax

        def _get_mu(x):
            bs, depth, h, w = x.shape
            ix = jnp.arange(1, h + 1, dtype=x.dtype).reshape(1, 1, h, 1)
            iy = jnp.arange(1, w + 1, dtype=x.dtype).reshape(1, 1, 1, w)
            sumX = jnp.maximum(x.sum((2, 3)), 1e-09)
            mu_x = jnp.maximum(jnp.round((ix * x).sum((2, 3)) / sumX), 1.0)
            mu_y = jnp.maximum(jnp.round((iy * x).sum((2, 3)) / sumX), 1.0)
            lin = jnp.linspace(-1.0, 1.0, h, dtype=x.dtype)
            mu_xg = lin[(mu_x - 1.0).astype(jnp.int32)]
            mu_yg = lin[(mu_y - 1.0).astype(jnp.int32)]
            return (mu_xg, mu_yg)

        def _get_mask(x, mask_weight, filt):
            bs, depth, h, w = x.shape
            mu_x, mu_y = _get_mu(x)
            posX = jnp.linspace(-1.0, 1.0, h, dtype=x.dtype).reshape(1, 1, h, 1)
            posY = jnp.linspace(-1.0, 1.0, w, dtype=x.dtype).reshape(1, 1, 1, w)
            m = jnp.abs(posX - mu_x[:, :, None, None]) + jnp.abs(posY - mu_y[:, :, None, None])
            m = 1.0 - m * mask_weight.reshape(1, depth, 1, 1)
            m = jnp.maximum(m, -1.0)
            m = jnp.where(filt.reshape(1, depth, 1, 1) == 1.0, m, 1.0)
            return m
        mask = _get_mask(x, mask_weight, filter)
        x_relu = jnp.maximum(x * mask, 0.0)
        out = lax.conv_general_dilated(x_relu, weight, window_strides=(1, 1), padding=[(padding, padding), (padding, padding)], dimension_numbers=('NCHW', 'OIHW', 'NCHW'))
        return out + bias.reshape(1, -1, 1, 1)

    def _gn(v, G=32, eps=1e-5):
        B_, C_, H_, W_ = v.shape
        g = v.reshape(B_, G, C_ // G, H_, W_)
        m = jnp.mean(g, axis=(2, 3, 4), keepdims=True)
        s = jnp.var(g, axis=(2, 3, 4), keepdims=True)
        return ((g - m) / jnp.sqrt(s + eps)).reshape(v.shape)

    def _ln_c(v, eps=1e-6):
        m = jnp.mean(v, axis=1, keepdims=True)
        s = jnp.var(v, axis=1, keepdims=True)
        return (v - m) / jnp.sqrt(s + eps)

    def _ln_t(v, eps=1e-5):
        m = jnp.mean(v, axis=-1, keepdims=True)
        s = jnp.var(v, axis=-1, keepdims=True)
        return (v - m) / jnp.sqrt(s + eps)

    def _to_tokens(v):
        B_, C_, H_, W_ = v.shape
        return v.reshape(B_, C_, H_ * W_).transpose(0, 2, 1)
    def _from_tokens(t, like):
        B_, C_, H_, W_ = like.shape
        return t.transpose(0, 2, 1).reshape(B_, C_, H_, W_)

    x = x + _L0_conv_ref(_gn(x), L0_conv_Wq, L0_conv_bq, L0_conv_Wk, L0_conv_bk, L0_conv_Wv, L0_conv_bv)
    x = x + _L1_conv_ref(_gn(x), L1_conv_weight, L1_conv_bias, L1_conv_mask_weight, L1_conv_filter, 1)
    return x


_drawn_inputs = setup_inputs


def setup_inputs(seed=0):
    import zlib

    import numpy as np

    out = dict(_drawn_inputs(seed))
    spreads = {'L1_conv_filter': (1.0, 0.2)}
    factors = {'L0_conv_bq': 50.886, 'L0_conv_bk': 38.867, 'L0_conv_bv': 8.0, 'L1_conv_bias': 3.924}
    for name, (base, spread) in spreads.items():
        noise = np.random.default_rng([zlib.crc32(name.encode()), seed]).standard_normal(out[name].shape)
        drawn = base * np.exp(spread * noise) if base else spread * noise
        out[name] = jnp.asarray(drawn.astype(out[name].dtype))
    for name, factor in factors.items():
        out[name] = (out[name] * factor).astype(out[name].dtype)
    return out
```

```python
from contextlib import ExitStack

import concourse.bass as bass
from concourse import mybir

F32 = mybir.dt.float32
F16 = mybir.dt.float16
I32 = mybir.dt.int32
ALU = mybir.AluOpType
ACT = mybir.ActivationFunctionType
AX = mybir.AxisListType

P = 128
B, C, HW = 8, 512, 32
S = HW * HW
NC = C // P
HALF = 512
TOK = 128
D = 64
SEG = C // D
HPI = S // TOK
HPH = HALF // TOK
GRP = 16
WSCALE = 256.0
EPS = 1e-5
ROUND = 12582912.0
MAGIC = float(0x5F3759DF)
UNITS = SEG
MAX_QUOTA = [3, 3, 3, 3, 3, 1, 0, 0]

C_ID, C_GRP, C_ONE, C_IOTA, C_POS, C_END = 0, 128, 256, 320, 352, 384
B_Q, B_K, B_CONV, B_MASKW, B_FILT = 0, 4, 8, 12, 16


class Count:

    def __init__(self, per):
        self.n, self.per, self.i, self.entry = 0, per, None, 0

    def loop(self, i):
        self.i, self.entry = i, self.n

    def done(self, passes):
        assert self.n - self.entry == self.per, (self.n - self.entry, self.per)
        self.i, self.n = None, self.entry + self.per * passes

    def value(self):
        return self.n if self.i is None else self.i * self.per + self.n


def ring_items(u, nxt, prev, v_units, stat):
    first = sum(MAX_QUOTA[:u])
    tiles = [("max", first + k) for k in range(MAX_QUOTA[u])] if nxt else []
    at = {"a": tiles[0:1], "b": tiles[1:2], "c": tiles[2:]}
    at["d"] = [("value", u // 2)] if v_units and u % 2 else []
    if stat and u in (5, 7):
        at["d"].append(("stat", (u - 5) // 2))
    if nxt and u == 6:
        at["d"].append(("shift", 0))
    if prev and u == 1:
        at["d"].append(("den", 0))
    return at


def build(nc, x, wqT, wkT, wvT, chan, bv, wc, const, out):
    x_img = x.rearrange("b (c p) s -> b p c s", p=P)
    out_img = out.rearrange("b (c p) s -> b p c s", p=P)
    x1 = nc.dram_tensor("x1_scratch", (B, C, S), F32, kind="Internal").ap()
    x1_img = x1.rearrange("b (c p) s -> b p c s", p=P)

    top = ExitStack()
    with top:
        def sem(name):
            return top.enter_context(nc.semaphore(name))

        def sb(stack, name, shape, dt):
            return stack.enter_context(nc.sbuf_tensor(name, shape, dt))

        cst = sb(top, "cst", [P, C_END], F32)
        prm = sb(top, "prm", [P, 20], F32)
        bn = sb(top, "bn", [P, NC, 2, 6], F32)
        mv = sb(top, "mv", [P, NC, 2], F32)
        gmv = sb(top, "gmv", [P, NC, 2], F32)
        dm = sb(top, "dm", [P, NC], F32)
        ve = sb(top, "ve", [P, NC], F32)
        nt = sb(top, "nt", [P, 2, NC], F32)
        rstd = sb(top, "rstd", [P, NC], F32)
        nbias = sb(top, "nbias", [P, NC], F32)
        ident = cst[:, C_ID:C_ID + P]
        grp = cst[:, C_GRP:C_GRP + P]
        ones = cst[:, C_ONE:C_ONE + D]

        bank = [top.enter_context(nc.psum_tensor(f"bank{k}", [P, 512], F32)) for k in range(8)]
        sc_bank = bank[0:4]
        v_ring = bank[4:6]
        pv_bank = bank[6]
        qk_bank = bank[7]

        s_const = sem("const_loaded")
        s_stat = sem("stat_step")
        s_passed = sem("passed")
        s1 = {n: sem(n) for n in (
            "w_loaded0", "w_loaded1", "w_hi_done", "w_split", "x_loaded", "xr_loaded0", "xr_loaded1", "kb_clear", "xn_ready", "xn_hi", "xn_split",
            "qk_ready", "qk_out", "qk_hi", "qk_split", "qk_moved", "ring_full", "ring_free",
            "min_done", "shift_sent", "shift_row", "scores_full", "exp_done", "pv_done", "sum0", "sum1",
            "recip_done", "o_done", "resid_done", "x1_stored", "value_out")}

        def statistics(dve, xin, step):
            def chain(ins):
                ins.then_inc(s_stat, 1)
                step.n += 1

            def sync():
                dve.wait_ge(s_stat, step.value())

            def moments(c):
                for k in range(2):
                    chain(dve.bn_stats(bn[:, c, k], xin[:, c, k * 512:(k + 1) * 512]))

            def aggregate():
                sync()
                dve.sem_inc(s_passed, 1)
                for c in range(NC):
                    chain(dve.bn_aggr(mv[:, c], bn[:, c]))

            def centre(src):
                chain(dve.tensor_copy(gmv[:].rearrange("p c k -> p (c k)"), src[:, 0:2 * NC]))
                sync()
                chain(dve.tensor_tensor(dm[:], mv[:, :, 0], gmv[:, :, 0], ALU.subtract))
                sync()
                chain(dve.tensor_tensor(dm[:], dm[:], dm[:], ALU.mult))

            def finish(src):
                chain(dve.scalar_tensor_tensor(out=ve[:], in0=src[:, 0:NC], scalar=EPS, in1=gmv[:, :, 1],
                                               op0=ALU.add, op1=ALU.add))
                sync()
                chain(dve.tensor_scalar(nt[:, 0].bitcast(I32), ve[:].bitcast(I32), 1, None,
                                        ALU.logical_shift_right))
                sync()
                chain(dve.tensor_scalar(rstd[:].bitcast(I32), nt[:, 0].bitcast(I32), -1.0, MAGIC,
                                        ALU.mult, ALU.add))
                for _ in range(4):
                    sync()
                    chain(dve.tensor_tensor(nt[:, 0], rstd[:], rstd[:], ALU.mult))
                    sync()
                    chain(dve.scalar_tensor_tensor(out=nt[:, 1], in0=nt[:, 0], scalar=-0.5, in1=ve[:],
                                                   op0=ALU.mult, op1=ALU.mult))
                    sync()
                    chain(dve.scalar_tensor_tensor(out=rstd[:], in0=nt[:, 1], scalar=1.5, in1=rstd[:],
                                                   op0=ALU.add, op1=ALU.mult))
                sync()
                chain(dve.scalar_tensor_tensor(out=nbias[:], in0=gmv[:, :, 0], scalar=-1.0, in1=rstd[:],
                                               op0=ALU.mult, op1=ALU.mult))
            return moments, aggregate, centre, finish

        STAT_STEPS = 2 * NC + NC + 3 + 3 + 12 + 1
        STAT_AGG = 3 * NC
        STAT_DEV = STAT_AGG + 3

        def statistics_sum(pe, dst, k):
            if k == 0:
                return pe.matmul(dst[:, 0:2 * NC], grp, mv[:].rearrange("p c k -> p (c k)"),
                                 start=True, stop=True)
            return pe.matmul(dst[:, 0:NC], grp, dm[:], start=True, stop=True)

        st1 = ExitStack()
        w_hi = sb(st1, "w_hi", [P, 3, NC, C], F16)
        w_lo = sb(st1, "w_lo", [P, 3, NC, C], F16)
        bv_row = sb(st1, "bv_row", [P, C], F32)
        xs = sb(st1, "xs", [P, NC, S], F32)
        xr = sb(st1, "xr", [P, 2, NC, HALF], F32)
        xn32 = sb(st1, "xn32", [P, 2, HALF], F32)
        xn_hi = sb(st1, "xn_hi", [P, 2, NC, HALF], F16)
        xn_lo = sb(st1, "xn_lo", [P, 2, NC, HALF], F16)
        qk32 = sb(st1, "qk32", [P, 2, HALF], F32)
        qk_hi = sb(st1, "qk_hi", [P, 2, NC, HALF], F16)
        qk_lo = sb(st1, "qk_lo", [P, 2, NC, HALF], F16)
        k_a = sb(st1, "k_a", [P, 2, SEG, HALF], F16)
        q_a = sb(st1, "q_a", [P, 2, SEG, HALF], F16)
        k_b = sb(st1, "k_b", [P, 2, SEG, HALF], F16)
        q_b = sb(st1, "q_b", [P, 2, SEG, HALF], F16)
        val = sb(st1, "val", [P, 2, HPH, C], F32)
        prob = sb(st1, "prob", [P, 8, 512], F32)
        psum_acc = sb(st1, "prob_sum", [P, 2, 2, 512], F32)
        nmax = sb(st1, "nmax", [P, SEG, 2], F32)
        nmin = sb(st1, "nmin", [P, SEG], F32)
        shift = sb(st1, "shift", [SEG, 2, TOK], F16)
        o_sb = sb(st1, "o_sb", [P, 512], F32)
        q_av = q_a[:].rearrange("p h (j e) t -> p h e j t", e=2)
        q_bv = q_b[:].rearrange("p h (j e) t -> p h e j t", e=2)
        stage = prob[:].rearrange("p (a k) n -> p a k n", a=2)

        PER_RING = HPI * (16 + 1 + 1) + 2 * HPH + 2

        def tokens(s):
            return s // HPH, slice((s % HPH) * TOK, (s % HPH + 1) * TOK)

        st1.close()
        st2 = top.enter_context(ExitStack())
        cw_hi = sb(st2, "cw_hi", [P, 9, NC, C], F16)
        cw_lo = sb(st2, "cw_lo", [P, 9, NC, C], F16)
        cstage = sb(st2, "cstage", [P, 2, NC, C], F32)
        PW = HW + 2
        xc = sb(st2, "xc", [P, 2, NC, S], F32)
        xn2 = sb(st2, "xn2", [P, NC, S], F32)
        msk = sb(st2, "msk", [P, S], F32)
        pad_hi = sb(st2, "pad_hi", [P, 2, NC, PW, PW], F16)
        pad_lo = sb(st2, "pad_lo", [P, 2, NC, PW, PW], F16)
        rows = sb(st2, "rows", [P, NC, HW], F32)
        cols = sb(st2, "cols", [P, NC, HW], F32)
        wrow = sb(st2, "wrow", [P, NC, HW], F32)
        wcol = sb(st2, "wcol", [P, NC, HW], F32)
        mxy = sb(st2, "mxy", [P, 4, NC], F32)
        mwf = sb(st2, "mwf", [P, NC], F32)
        y_sb = sb(st2, "y_sb", [P, 2, 512], F32)
        s2 = {n: sem(n) for n in (
            "cw_loaded0", "cw_loaded1", "cw_hi_done", "cw_split", "pad_clear", "xc_loaded0", "xc_loaded1", "mask_step", "pad_ready", "sum2_full", "sum2_free",
            "conv_full", "conv_free", "y_out", "y_done", "y_stored0", "y_stored1")}
        MASK_STEPS = 3 * NC + 3 + 3 + 1 + 2 + 3 + 6 + 1 + 5 * NC

        block = top.enter_context(nc.Block())

        @block.sync
        def _(sp):
            sp.dma_start(cst[:], const).then_inc(s_const, 16)
            sp.dma_start(prm[:], chan).then_inc(s_const, 16)
            sp.dma_start(bv_row[:], bv.partition_broadcast(P)).then_inc(s_const, 16)
            sp.dma_start(xs[:], x_img[0]).then_inc(s1["x_loaded"], 16)
            for k, w in enumerate((wqT, wkT, wvT)):
                if k == 2:
                    sp.wait_ge(s1["w_split"], 1)
                sp.dma_start(stage[:, k % 2], w.rearrange("(c p) n -> p c n", p=P)).then_inc(s1[f"w_loaded{k % 2}"], 16)
            sp.dma_start(xr[:, 0], x_img[0][:, :, 0:HALF]).then_inc(s1["xr_loaded0"], 16)

            def move_qk(which, t, half, first=False):
                sp.wait_ge(s1["qk_split"], 2 + 8 * t + 4 * (which + 1))
                if not first:
                    sp.sem_inc(s_passed, 1)
                    sp.wait_ge(s1["exp_done"], 4 + 64 * (t - 1))
                hi_to = ((k_a, 0), (k_b, 0)) if which == 0 else ((q_a, 0), (q_a, D))
                lo_to = (k_a, D) if which == 0 else (q_b, 0)
                for e in range(2):
                    src = slice(e * D, (e + 1) * D)
                    for dst, p0 in hi_to:
                        sp.dma_start(dst[p0:p0 + D, half, e::2, :], qk_hi[src, which]).then_inc(s1["qk_moved"], 16)
                    dst, p0 = lo_to
                    sp.dma_start(dst[p0:p0 + D, half, e::2, :], qk_lo[src, which]).then_inc(s1["qk_moved"], 16)

            def send_shift(h, s):
                half, tok = tokens(s)
                sp.wait_ge(s1["shift_sent"], h + 1)
                sp.dma_start(q_b[D:D + 1, half, :, tok], shift[:, s % 2]).then_inc(s1["shift_row"], 16)

            def store_x1(t, img, half):
                sp.wait_ge(s1["resid_done"], 1 + 4 * (t + 1))
                sp.sem_inc(s_passed, 1)
                sp.dma_start(x1_img[img][:, :, half * HALF:(half + 1) * HALF], xr[:, half]).then_inc(s1["x1_stored"], 16)

            def slot(img, s, prev=True, nxt=True, more=True):
                t = img * 2 + s // HPH
                r = s % HPH
                if r == 1 and (s < HPH or more):
                    move_qk(0, t + 1, 1 - s // HPH)
                if r == 2 and (s < HPH or more):
                    move_qk(1, t + 1, 1 - s // HPH)
                if r == 1 and (s < HPH or more):
                    sp.wait_ge(s1["x1_stored"], 16 + 16 * t)
                    if s < HPH:
                        src = x_img[img][:, :, HALF:S]
                    else:
                        src = x_img[img + 1][:, :, 0:HALF]
                    sp.dma_start(xr[:, 1 - s // HPH], src).then_inc(s1[f"xr_loaded{1 - s // HPH}"], 16)
                if s == 1 and more:
                    sp.wait_ge(s1["xn_ready"], 8 * (img + 1))
                    sp.dma_start(xs[:], x_img[img + 1]).then_inc(s1["x_loaded"], 16)
                if nxt:
                    send_shift(img * HPI + s + 1, (s + 1) % HPI)
                if r == 0 and prev:
                    if s == 0:
                        store_x1(t - 1, img - 1, 1)
                    else:
                        store_x1(t - 1, img, 0)

            sp.sem_inc(s1["x1_stored"], 16)
            sp.wait_ge(s1["kb_clear"], 6)
            move_qk(0, 0, 0, first=True)
            move_qk(1, 0, 0, first=True)
            send_shift(0, 0)
            slot(0, 0, prev=False)
            with sp.Fori(0, B - 1) as i:
                for s in range(1, HPI):
                    slot(i, s)
                slot(i + 1, 0)
            for s in range(1, HPI):
                slot(B - 1, s, nxt=s < HPI - 1, more=False)
            store_x1(2 * B - 1, B - 1, 1)
            sp.wait_ge(s1["x1_stored"], 16 + 16 * 2 * B)

            for k in range(9):
                if k >= 2:
                    sp.wait_ge(s2["cw_split"], k - 1)
                sp.dma_start(cstage[:, k % 2], wc[k].rearrange("(c p) n -> p c n", p=P)).then_inc(s2[f"cw_loaded{k % 2}"], 16)
            with sp.Fori(0, B // 2) as j:
                for b in range(2):
                    img = j * 2 + b
                    sp.wait_ge(s2["y_done"], 1 + img * 8)
                    sp.dma_start(xc[:, b], x1_img[img]).then_inc(s2[f"xc_loaded{b}"], 16)

        @block.tensor
        def _(pe):
            ring = Count(PER_RING)

            def take():
                pe.wait_ge(s1["ring_free"], ring.value() + 1)
                dst = v_ring[ring.n % 2]
                ring.n += 1
                return dst

            def stat_item(img, k):
                dst = take()
                pe.wait_ge(s_stat, img * STAT_STEPS + (STAT_AGG, STAT_DEV)[k])
                statistics_sum(pe, dst, k).then_inc(s1["ring_full"], 1)

            def project_qk(t, half, which, j):
                w = 1 - which
                pe.wait_ge(s1["xn_split"], 2 + 4 * (t + 1))
                pe.wait_ge(s1["qk_out"], 8 * t + 4 * which + j + 1)
                steps = [(a, b, c) for c in range(NC) for a, b in
                         ((w_hi, xn_hi), (w_hi, xn_lo), (w_lo, xn_hi))]
                for n, (a, b, c) in enumerate(steps):
                    mm = pe.matmul(qk_bank[:], a[:, w, c, j * P:(j + 1) * P], b[:, half, c],
                                   start=(n == 0), stop=(n == len(steps) - 1))
                mm.then_inc(s1["qk_ready"], 1)

            def project_value(t, half, g):
                pe.wait_ge(s1["xn_split"], 2 + 4 * (t + 1))
                dst = take()
                steps = [(a, b, c) for c in range(NC) for a, b in
                         ((xn_hi, w_hi), (xn_hi, w_lo), (xn_lo, w_hi))]
                for n, (a, b, c) in enumerate(steps):
                    mm = pe.matmul(dst[:], a[:, half, c, g * TOK:(g + 1) * TOK], b[:, 2, c],
                                   start=(n == 0), stop=(n == len(steps) - 1))
                mm.then_inc(s1["ring_full"], 1)

            def max_tile(s, m):
                half, tok = tokens(s)
                dst = take()
                pe.matmul(dst[:].rearrange("p (k t) -> p k t", t=TOK), q_a[:, half, m // 2, tok],
                          k_a[:, half, 4 * (m % 2):4 * (m % 2) + 4, tok],
                          start=True, stop=True).then_inc(s1["ring_full"], 1)

            def shift_item(h):
                dst = take()
                pe.wait_ge(s1["min_done"], h + 1)
                pe.matmul(dst[0:SEG, 0:TOK], nmin[:], ident, start=True, stop=True).then_inc(s1["ring_full"], 1)

            def den_item(h, par):
                dst = take()
                pe.wait_ge(s1["sum0"], 7 + 7 * (h + 1))
                pe.matmul(dst[0:D, :], ones, psum_acc[:, par, 0], start=True, stop=True)
                pe.wait_ge(s1["sum1"], 7 + 7 * (h + 1))
                pe.matmul(dst[D:P, :], ones, psum_acc[:, par, 1], start=True, stop=True).then_inc(s1["ring_full"], 1)

            def scores(h, s, u, part):
                half, tok = tokens(s)
                k_op, q_op = ((k_a, q_av), (k_b, q_bv))[part]
                for e in range(2):
                    b = (s * 16 + u * 2 + e) % 4
                    if part == 0:
                        pe.wait_ge(s1["exp_done"], 16 * h + 2 * u + e + 1)
                    mm = pe.matmul(sc_bank[b][:].rearrange("p (j t) -> p j t", t=TOK), k_op[:, half, u, tok],
                                   q_op[:, half, e, :, tok], start=(part == 0), stop=(part == 1))
                    if part == 1:
                        mm.then_inc(s1["scores_full"], 1)

            def weigh(h, s, kc):
                if kc == 0:
                    pe.wait_ge(s1["o_done"], h + 1)
                    pe.wait_ge(s1["value_out"], h + 1)
                for e in range(2):
                    pe.wait_ge(s1["exp_done"], 4 + 16 * h + 2 * kc + e + 1)
                    pe.matmul(pv_bank[e * D:(e + 1) * D, :], val[:, s // HPH, s % HPH, kc * D:(kc + 1) * D],
                              prob[:, (2 * kc + e) % 8], start=(kc == 0),
                              stop=(kc == SEG - 1)).then_inc(s1["pv_done"], 1)

            def slot(img, s, prev=True, nxt=True, more=True):
                h = img * HPI + s
                t = img * 2 + s // HPH
                r = s % HPH
                proj = r < 3 and (s < HPH or more)
                for u in range(UNITS):
                    items = ring_items(u, nxt, prev, proj and r == 2, s == 2 and more)

                    def run(place):
                        for kind, a in items[place]:
                            if kind == "max":
                                max_tile((s + 1) % HPI, a)
                            elif kind == "value":
                                project_value(t + 1, 1 - s // HPH, a)
                            elif kind == "stat":
                                stat_item(img + 1, a)
                            elif kind == "shift":
                                shift_item(h + 1)
                            else:
                                den_item(h - 1, (s - 1) % 2)
                    if u == 0 and nxt and r == 3:
                        pe.wait_ge(s1["qk_moved"], 192 * (t + 2))
                    run("a")
                    scores(h, s, u, 0)
                    run("b")
                    if u == 0:
                        pe.wait_ge(s1["shift_row"], 16 * (h + 1))
                    scores(h, s, u, 1)
                    run("c")
                    if proj and r < 2 and u % 2:
                        project_qk(t + 1, 1 - s // HPH, r, u // 2)
                    run("d")
                    if u == 0 and prev:
                        weigh(h - 1, (s - 1) % HPI, SEG - 1)
                    if u == 2:
                        weigh(h, s, 0)
                    if u >= 2:
                        weigh(h, s, u - 1)

            pe.sem_inc(s1["pv_done"], 8)
            pe.wait_ge(s_const, 48)
            stat_item(0, 0)
            stat_item(0, 1)
            pe.wait_ge(s1["w_split"], 3)
            for which in range(2):
                for j in range(NC):
                    project_qk(0, 0, which, j)
            for g in range(HPH):
                project_value(0, 0, g)
            pe.wait_ge(s1["qk_moved"], 192)
            for m in range(16):
                max_tile(0, m)
            shift_item(0)
            slot(0, 0, prev=False)
            with pe.Fori(0, B - 1) as i:
                ring.loop(i)
                for s in range(1, HPI):
                    slot(i, s)
                slot(i + 1, 0)
            ring.done(B - 1)
            for s in range(1, HPI):
                slot(B - 1, s, nxt=s < HPI - 1, more=False)
            weigh(B * HPI - 1, HPI - 1, SEG - 1)
            den_item(B * HPI - 1, 1)

            pe.wait_ge(s1["o_done"], B * HPI + 1)
            pe.sem_inc(s2["conv_full"], 9)
            with pe.Fori(0, B // 2) as j:
                for b in range(2):
                    img = j * 2 + b
                    for k in range(2):
                        pe.wait_ge(s2["sum2_free"], img * 2 + k + 1)
                        pe.wait_ge(s_stat, STAT_STEPS * B + img * STAT_STEPS + (STAT_AGG, STAT_DEV)[k])
                        statistics_sum(pe, qk_bank, k).then_inc(s2["sum2_full"], 1)
                    pe.wait_ge(s2["cw_split"], 9)
                    pe.wait_ge(s2["pad_ready"], img + 1)
                    for k in range(8):
                        co, hf = k // 2, k % 2
                        pe.wait_ge(s2["conv_free"], img * 8 + k + 1)
                        steps = [(tap, c, a, v) for tap in range(9) for c in range(NC) for a, v in
                                 ((cw_hi, pad_hi), (cw_hi, pad_lo), (cw_lo, pad_hi))]
                        for n, (tap, c, a, v) in enumerate(steps):
                            ky, kx = tap // 3, tap % 3
                            r0 = hf * (HW // 2) + ky
                            mm = pe.matmul(bank[k % 4][:].rearrange("p (r q) -> p r q", q=HW),
                                           a[:, tap, c, co * P:(co + 1) * P],
                                           v[:, b, c, r0:r0 + HW // 2, kx:kx + HW],
                                           start=(n == 0), stop=(n == len(steps) - 1))
                        mm.then_inc(s2["conv_full"], 1)

        @block.scalar
        def _(act):
            def normed(img, half, c):
                k = 4 * half + c
                act.wait_ge(s_stat, (img + 1) * STAT_STEPS)
                act.wait_ge(s1["xn_split"], img * 8 + k + 1)
                act.activation(xn32[:, c % 2], xs[:, c, half * HALF:(half + 1) * HALF], ACT.Identity,
                               bias=nbias[:, c:c + 1], scale=rstd[:, c:c + 1]).then_inc(s1["xn_ready"], 1)

            def qk_evacuate(t, which, j):
                act.wait_ge(s1["qk_ready"], 8 * t + 4 * which + j + 1)
                act.wait_ge(s1["qk_split"], 8 * t + 4 * which + j + 1)
                col = (B_K, B_Q)[which] + j
                act.activation(qk32[:, j % 2], qk_bank[:], ACT.Identity, bias=prm[:, col:col + 1],
                               scale=1.0 / WSCALE).then_inc(s1["qk_out"], 1)

            def exp_tile(h, u, e):
                act.wait_ge(s1["scores_full"], 16 * h + 2 * u + e + 1)
                act.wait_ge(s1["pv_done"], 16 * h + 2 * u + e + 1)
                act.wait_ge(s1[f"sum{e}"], 7 * h + (u + 4 if u < 4 else 7 + max(u - 4, 1)))
                act.activation(prob[:, (2 * u + e) % 8], sc_bank[(2 * u + e) % 4][:], ACT.Exp,
                               scale=float(D) ** -0.5).then_inc(s1["exp_done"], 1)

            def slot(img, s, more=True):
                h = img * HPI + s
                t = img * 2 + s // HPH
                r = s % HPH
                for u in range(UNITS):
                    exp_tile(h, u, 0)
                    exp_tile(h, u, 1)
                    if r < 2 and u % 2 and (s < HPH or more):
                        qk_evacuate(t + 1, r, u // 2)
                    if s == 3 and more and 1 <= u < 5:
                        normed(img + 1, 0, u - 1)
                    if s == 4 and more and u < 4:
                        normed(img + 1, 1, u)

            act.sem_inc(s1["exp_done"], 4)
            act.sem_inc(s1["qk_out"], 1)
            act.wait_ge(s_const, 48)
            for half in range(2):
                for c in range(NC):
                    normed(0, half, c)
            for which in range(2):
                for j in range(NC):
                    qk_evacuate(0, which, j)
            slot(0, 0)
            with act.Fori(0, B - 1) as i:
                for s in range(1, HPI):
                    slot(i, s)
                slot(i + 1, 0)
            for s in range(1, HPI):
                slot(B - 1, s, more=False)

            act.sem_inc(s2["conv_free"], 4)
            act.sem_inc(s2["y_stored0"], 16)
            act.sem_inc(s2["y_stored1"], 16)
            with act.Fori(0, B // 2) as j:
                for b in range(2):
                    img = j * 2 + b
                    for k in range(8):
                        act.wait_ge(s2["conv_full"], 9 + img * 8 + k + 1)
                        act.wait_ge(s2[f"y_stored{k % 2}"], 16 + img * 64 + 16 * (k // 2))
                        act.activation(y_sb[:, k % 2], bank[k % 4][:], ACT.Identity,
                                       bias=prm[:, B_CONV + k // 2:B_CONV + k // 2 + 1],
                                       scale=1.0 / WSCALE).then_inc(s2["y_out"], 1)
                        act.wait_ge(s2["y_out"], img * 8 + k + 1)
                        act.sem_inc(s2["conv_free"], 1)
                        act.wait_ge(s2["y_done"], 9 + img * 8 + k + 1)
                        act.dma_start(out_img[img][:, k // 2, (k % 2) * 512:(k % 2 + 1) * 512],
                                      y_sb[:, k % 2]).then_inc(s2[f"y_stored{k % 2}"], 16)
            for k in range(2):
                act.wait_ge(s2[f"y_stored{k}"], 16 + 16 * 4 * B)

        @block.gpsimd
        def _(pool):
            def add_tile(h, s, kc):
                pool.wait_ge(s1["exp_done"], 4 + 16 * h + 2 * kc + 2)
                acc = psum_acc[:, s % 2, 1]
                pool.wait_ge(s1["sum1"], 7 + 7 * h + kc - 1)
                in0 = prob[:, 1] if kc == 1 else acc
                nc.gpsimd.tensor_tensor(acc, in0, prob[:, (2 * kc + 1) % 8], ALU.add).then_inc(s1["sum1"], 1)

            def residual(h, s):
                half, tok = tokens(s)
                pool.wait_ge(s1["o_done"], 1 + h + 1)
                o_v = o_sb[:].rearrange("p (j t) -> p j t", t=TOK)
                nc.gpsimd.tensor_tensor(xr[:, half, :, tok], xr[:, half, :, tok], o_v, ALU.add)\
                    .then_inc(s1["resid_done"], 1)

            def slot(img, s, prev=True):
                h = img * HPI + s
                for u in range(UNITS):
                    if u == 0 and prev:
                        add_tile(h - 1, (s - 1) % HPI, SEG - 1)
                    if u >= 2:
                        add_tile(h, s, u - 1)
                    if u == 2 and prev:
                        if s % HPH == 1:
                            pool.wait_ge(s1[f"xr_loaded{s // HPH}"], 16 * (img + 1))
                        residual(h - 1, (s - 1) % HPI)

            nc.gpsimd.memset(k_b[D:P], 0.0).then_inc(s1["kb_clear"], 1)
            nc.gpsimd.memset(q_b[D:P], 0.0).then_inc(s1["kb_clear"], 1)
            pool.wait_ge(s1["kb_clear"], 2)
            nc.gpsimd.memset(k_b[D:D + 1], 8.0).then_inc(s1["kb_clear"], 4)
            pool.sem_inc(s1["sum1"], 7)
            pool.sem_inc(s1["resid_done"], 1)
            slot(0, 0, prev=False)
            with pool.Fori(0, B - 1) as i:
                for s in range(1, HPI):
                    slot(i, s)
                slot(i + 1, 0)
            for s in range(1, HPI):
                slot(B - 1, s)
            add_tile(B * HPI - 1, HPI - 1, SEG - 1)
            residual(B * HPI - 1, HPI - 1)

            pool.wait_ge(s1["x1_stored"], 16 + 16 * 2 * B)
            nc.gpsimd.memset(pad_lo[:], 0.0).then_inc(s2["pad_clear"], 1)
            pool.sem_inc(s2["y_done"], 9)
            with pool.Fori(0, B // 2) as j:
                for b in range(2):
                    img = j * 2 + b
                    pool.wait_ge(s2[f"xc_loaded{b}"], 16 * (j + 1))
                    for k in range(8):
                        co, hf = k // 2, k % 2
                        pool.wait_ge(s2["y_out"], img * 8 + k + 1)
                        nc.gpsimd.tensor_tensor(y_sb[:, k % 2], y_sb[:, k % 2],
                                                xc[:, b, co, hf * 512:(hf + 1) * 512], ALU.add)\
                            .then_inc(s2["y_done"], 1)

        @block.vector
        def _(dve):
            ring = Count(PER_RING)
            step = Count(STAT_STEPS)

            def item():
                dve.wait_ge(s1["ring_full"], ring.value() + 1)
                src = v_ring[ring.n % 2]
                ring.n += 1
                return src

            moments, aggregate, centre, finish = statistics(dve, xs, step)

            def split_norm(img, half, c):
                k = 4 * half + c
                dve.wait_ge(s1["xn_ready"], img * 8 + k + 1)
                dve.tensor_copy(xn_hi[:, half, c], xn32[:, c % 2]).then_inc(s1["xn_hi"], 1)
                dve.wait_ge(s1["xn_hi"], img * 8 + k + 1)
                dve.tensor_tensor(xn_lo[:, half, c], xn32[:, c % 2], xn_hi[:, half, c], ALU.subtract)\
                    .then_inc(s1["xn_split"], 1)

            def split_qk(t, which, j):
                n = 8 * t + 4 * which + j
                dve.wait_ge(s1["qk_out"], 1 + n + 1)
                if j == 0:
                    dve.wait_ge(s1["qk_moved"], 192 * t)
                dve.tensor_copy(qk_hi[:, which, j], qk32[:, j % 2]).then_inc(s1["qk_hi"], 1)
                dve.wait_ge(s1["qk_hi"], n + 1)
                dve.tensor_tensor(qk_lo[:, which, j], qk32[:, j % 2], qk_hi[:, which, j], ALU.subtract)\
                    .then_inc(s1["qk_split"], 1)

            def add_tile(h, s, kc):
                dve.wait_ge(s1["exp_done"], 4 + 16 * h + 2 * kc + 1)
                acc = psum_acc[:, s % 2, 0]
                dve.wait_ge(s1["sum0"], 7 + 7 * h + kc - 1)
                in0 = prob[:, 0] if kc == 1 else acc
                dve.tensor_tensor(acc, in0, prob[:, (2 * kc) % 8], ALU.add).then_inc(s1["sum0"], 1)

            def max_item(h, m):
                src = item()
                if m == 0:
                    dve.wait_ge(s1["min_done"], h)
                dve.tensor_reduce(nmax[:, m // 2, m % 2:m % 2 + 1], src[:], AX.X, ALU.max, negate=True)\
                    .then_inc(s1["ring_free"], 1)
                if m == 15:
                    dve.wait_ge(s1["ring_free"], 2 + ring.value())
                    dve.tensor_tensor(nmin[:], nmax[:, :, 0], nmax[:, :, 1], ALU.min).then_inc(s1["min_done"], 1)

            def shift_item(h, s):
                src = item()
                if s > 0:
                    dve.wait_ge(s1["shift_row"], 16 * (h - 1))
                dve.tensor_scalar(shift[:, s % 2], src[0:SEG, 0:TOK], 0.125, None, ALU.mult)\
                    .then_inc(s1["shift_sent"], 1)
                dve.wait_ge(s1["shift_sent"], h + 1)
                dve.sem_inc(s1["ring_free"], 1)

            def value_item(h, half, g):
                src = item()
                dve.scalar_tensor_tensor(out=val[:, half, g], in0=src[:], scalar=1.0 / WSCALE, in1=bv_row[:],
                                         op0=ALU.mult, op1=ALU.add).then_inc(s1["value_out"], 1)
                dve.wait_ge(s1["value_out"], h + 1)
                dve.sem_inc(s1["ring_free"], 1)

            def den_item(h, s):
                src = item()
                dve.wait_ge(s1["resid_done"], h + 1)
                dve.reciprocal(o_sb[:], src[:]).then_inc(s1["ring_free"], 1)
                dve.wait_ge(s1["ring_free"], 2 + ring.value())
                dve.wait_ge(s1["pv_done"], 8 + 16 * (h + 1))
                dve.tensor_tensor(o_sb[:], pv_bank[:], o_sb[:], ALU.mult).then_inc(s1["o_done"], 1)

            def stat_item(img, k):
                src = item()
                (centre, finish)[k](src)
                dve.wait_ge(s_stat, step.value())
                dve.sem_inc(s1["ring_free"], 1)

            def slot(img, s, prev=True, nxt=True, more=True):
                h = img * HPI + s
                t = img * 2 + s // HPH
                r = s % HPH
                proj = r < 3 and (s < HPH or more)
                for u in range(UNITS):
                    if u == 0 and prev:
                        add_tile(h - 1, (s - 1) % HPI, SEG - 1)
                    if u >= 2:
                        add_tile(h, s, u - 1)
                    if s == 2 and more:
                        if u == 0:
                            dve.wait_ge(s1["x_loaded"], 16 * (img + 2))
                        if u < 4:
                            moments(u)
                        if u == 4:
                            aggregate()
                    items = ring_items(u, nxt, prev, proj and r == 2, s == 2 and more)
                    for place in "abcd":
                        for kind, a in items[place]:
                            if kind == "max":
                                max_item(h + 1, a)
                            elif kind == "value":
                                value_item(4 * (t + 1) + a, 1 - s // HPH, a)
                            elif kind == "stat":
                                stat_item(img + 1, a)
                            elif kind == "shift":
                                shift_item(h + 1, s + 1)
                            else:
                                den_item(h - 1, s - 1)
                    if s < HPH or more:
                        if r == 0 and u in (2, 4, 6):
                            split_qk(t + 1, 0, u // 2 - 1)
                        if r == 1:
                            if u == 0:
                                split_qk(t + 1, 0, 3)
                            if u in (2, 4, 6):
                                split_qk(t + 1, 1, u // 2 - 1)
                        if r == 2 and u == 0:
                            split_qk(t + 1, 1, 3)
                    if s == 3 and more and 2 <= u < 6:
                        split_norm(img + 1, 0, u - 2)
                    if s == 4 and more and 1 <= u < 5:
                        split_norm(img + 1, 1, u - 1)

            for name, credit in (("ring_free", 2), ("sum0", 7), ("o_done", 1), ("qk_split", 2), ("xn_split", 2)):
                dve.sem_inc(s1[name], credit)
            dve.wait_ge(s1["x_loaded"], 16)
            for c in range(NC):
                moments(c)
            aggregate()
            dve.wait_ge(s_const, 48)
            stat_item(0, 0)
            stat_item(0, 1)
            for k in range(3):
                dve.wait_ge(s1[f"w_loaded{k % 2}"], 16 * (k // 2 + 1))
                hi, lo = (t_[:, k].rearrange("p c n -> p (c n)") for t_ in (w_hi, w_lo))
                src = stage[:, k % 2].rearrange("p c n -> p (c n)")
                dve.tensor_scalar(hi, src, WSCALE, None, ALU.mult).then_inc(s1["w_hi_done"], 1)
                dve.wait_ge(s1["w_hi_done"], k + 1)
                dve.scalar_tensor_tensor(out=lo, in0=src, scalar=WSCALE, in1=hi,
                                         op0=ALU.mult, op1=ALU.subtract).then_inc(s1["w_split"], 1)
            for half in range(2):
                for c in range(NC):
                    split_norm(0, half, c)
            for which in range(2):
                for j in range(NC):
                    split_qk(0, which, j)
            for g in range(HPH):
                value_item(g, 0, g)
            for m in range(16):
                max_item(0, m)
            shift_item(0, 0)
            slot(0, 0, prev=False)
            with dve.Fori(0, B - 1) as i:
                ring.loop(i)
                step.loop(i)
                for s in range(1, HPI):
                    slot(i, s)
                slot(i + 1, 0)
            ring.done(B - 1)
            step.done(B - 1)
            for s in range(1, HPI):
                slot(B - 1, s, nxt=s < HPI - 1, more=False)
            add_tile(B * HPI - 1, HPI - 1, SEG - 1)
            den_item(B * HPI - 1, HPI - 1)

            dve.wait_ge(s1["x1_stored"], 16 + 16 * 2 * B)
            dve.sem_inc(s2["sum2_free"], 1)
            dve.memset(pad_hi[:], 0.0).then_inc(s2["pad_clear"], 1)
            for k in range(9):
                dve.wait_ge(s2[f"cw_loaded{k % 2}"], 16 * (k // 2 + 1))
                hi, lo = (t_[:, k].rearrange("p c n -> p (c n)") for t_ in (cw_hi, cw_lo))
                src = cstage[:, k % 2].rearrange("p c n -> p (c n)")
                dve.tensor_scalar(hi, src, WSCALE, None, ALU.mult).then_inc(s2["cw_hi_done"], 1)
                dve.wait_ge(s2["cw_hi_done"], k + 1)
                dve.scalar_tensor_tensor(out=lo, in0=src, scalar=WSCALE, in1=hi,
                                         op0=ALU.mult, op1=ALU.subtract).then_inc(s2["cw_split"], 1)
            dve.wait_ge(s2["pad_clear"], 2)
            dve.tensor_scalar(mwf[:], prm[:, B_FILT:B_FILT + NC], 1.0, None, ALU.is_equal).then_inc(s2["mask_step"], 1)
            dve.wait_ge(s2["mask_step"], 1)
            dve.tensor_tensor(mwf[:], mwf[:], prm[:, B_MASKW:B_MASKW + NC], ALU.mult).then_inc(s2["mask_step"], 1)
            mstep = Count(2 * MASK_STEPS)
            mstep.n = 2
            step.per = 2 * STAT_STEPS

            def chain(ins):
                ins.then_inc(s2["mask_step"], 1)
                mstep.n += 1

            def sync():
                dve.wait_ge(s2["mask_step"], mstep.value())

            iota = cst[:, C_IOTA:C_IOTA + HW].unsqueeze(1).broadcast_to([P, NC, HW])
            place = cst[:, C_POS:C_POS + HW].unsqueeze(1).broadcast_to([P, NC, HW])

            def over_hw(v):
                return v.unsqueeze(2).broadcast_to([P, NC, HW])

            with dve.Fori(0, B // 2) as j:
                step.loop(j)
                mstep.loop(j)
                for b in range(2):
                    img = j * 2 + b
                    dve.wait_ge(s2[f"xc_loaded{b}"], 16 * (j + 1))
                    moments, aggregate, centre, finish = statistics(dve, xc[:, b], step)
                    for c in range(NC):
                        moments(c)
                    aggregate()
                    for k, part in enumerate((centre, finish)):
                        dve.wait_ge(s2["sum2_full"], img * 2 + k + 1)
                        part(qk_bank)
                        dve.wait_ge(s_stat, step.value())
                        dve.sem_inc(s2["sum2_free"], 1)
                    for c in range(NC):
                        chain(dve.tensor_scalar(xn2[:, c], xc[:, b, c], rstd[:, c:c + 1], nbias[:, c:c + 1],
                                                ALU.mult, ALU.add))
                    sync()
                    for c in range(NC):
                        v = xn2[:, c].rearrange("p (h w) -> p h w", w=HW)
                        chain(dve.tensor_reduce(rows[:, c], v, AX.X, ALU.add))
                        chain(dve.tensor_reduce(cols[:, c], v.rearrange("p h w -> p w h"), AX.X, ALU.add))
                    sync()
                    chain(dve.tensor_tensor(wrow[:], rows[:], iota, ALU.mult))
                    chain(dve.tensor_tensor(wcol[:], cols[:], iota, ALU.mult))
                    chain(dve.tensor_reduce(mxy[:, 2], rows[:], AX.X, ALU.add))
                    sync()
                    chain(dve.tensor_reduce(mxy[:, 0], wrow[:], AX.X, ALU.add))
                    chain(dve.tensor_reduce(mxy[:, 1], wcol[:], AX.X, ALU.add))
                    chain(dve.tensor_scalar(mxy[:, 2], mxy[:, 2], 1e-9, None, ALU.max))
                    sync()
                    chain(dve.reciprocal(mxy[:, 3], mxy[:, 2]))
                    sync()
                    for a in range(2):
                        chain(dve.tensor_tensor(mxy[:, a], mxy[:, a], mxy[:, 3], ALU.mult))
                    sync()
                    chain(dve.tensor_scalar(mxy[:, 0:2], mxy[:, 0:2], 1.0, float(HW), ALU.max, ALU.min))
                    sync()
                    chain(dve.tensor_scalar(mxy[:, 0:2], mxy[:, 0:2], ROUND, ROUND, ALU.add, ALU.subtract))
                    sync()
                    chain(dve.tensor_scalar(mxy[:, 0:2], mxy[:, 0:2], 2.0 / (HW - 1), -1.0 - 2.0 / (HW - 1),
                                            ALU.mult, ALU.add))
                    sync()
                    for a, w in enumerate((wrow, wcol)):
                        chain(dve.tensor_tensor(w[:], place, over_hw(mxy[:, a]), ALU.subtract))
                    sync()
                    for w in (wrow, wcol):
                        chain(dve.scalar_tensor_tensor(out=w[:], in0=w[:], scalar=-1.0, in1=w[:],
                                                       op0=ALU.mult, op1=ALU.max))
                    sync()
                    for w in (wrow, wcol):
                        chain(dve.tensor_tensor(w[:], w[:], over_hw(mwf[:]), ALU.mult))
                    sync()
                    chain(dve.tensor_scalar(wrow[:], wrow[:], -1.0, 1.0, ALU.mult, ALU.add))
                    dve.wait_ge(s2["conv_full"], 1 + img * 8)
                    for c in range(NC):
                        sync()
                        m3 = msk[:].rearrange("p (h w) -> p h w", w=HW)
                        chain(dve.tensor_tensor(m3, wrow[:, c].unsqueeze(2).broadcast_to([P, HW, HW]),
                                                wcol[:, c].unsqueeze(1).broadcast_to([P, HW, HW]), ALU.subtract))
                        sync()
                        chain(dve.scalar_tensor_tensor(out=msk[:], in0=msk[:], scalar=-1.0, in1=xn2[:, c],
                                                       op0=ALU.max, op1=ALU.mult))
                        sync()
                        chain(dve.tensor_scalar(msk[:], msk[:], 0.0, None, ALU.max))
                        sync()
                        inner = (slice(None), b, c, slice(1, HW + 1), slice(1, HW + 1))
                        chain(dve.tensor_copy(pad_hi[inner], m3))
                        sync()
                        chain(dve.tensor_tensor(pad_lo[inner], m3, pad_hi[inner], ALU.subtract))
                    sync()
                    dve.sem_inc(s2["pad_ready"], 1)
            step.done(B // 2)
            mstep.done(B // 2)


_INS = ["x", "wqT", "wkT", "wvT", "chan", "bv", "wc", "const"]


def constants(np):
    c = np.zeros((P, C_END), np.float32)
    c[:, C_ID:C_ID + P] = np.eye(P)
    c[:, C_GRP:C_GRP + P] = np.kron(np.eye(P // GRP), np.full((GRP, GRP), 1.0 / GRP))
    c[:, C_ONE:C_ONE + D] = 1.0
    c[:, C_IOTA:C_IOTA + HW] = np.arange(1, HW + 1)
    c[:, C_POS:C_POS + HW] = np.linspace(-1.0, 1.0, HW)
    return c


def kernel(**inputs):
    import numpy as np
    import concourse.bacc as bacc
    from concourse.bass_utils import run_bass_kernel_spmd

    a = {k: np.asarray(v) for k, v in inputs.items()}
    column = [a[k].reshape(NC, P).T for k in
              ("L0_conv_bq", "L0_conv_bk", "L1_conv_bias", "L1_conv_mask_weight", "L1_conv_filter")]
    arrays = {
        "x": a["x"].reshape(B, C, S),
        "wqT": a["L0_conv_Wq"].T,
        "wkT": a["L0_conv_Wk"].T,
        "wvT": a["L0_conv_Wv"].T,
        "chan": np.concatenate(column, axis=1),
        "bv": a["L0_conv_bv"],
        "wc": a["L1_conv_weight"].transpose(2, 3, 1, 0).reshape(9, C, C),
        "const": constants(np),
    }
    arrays = {k: np.ascontiguousarray(v) for k, v in arrays.items()}
    nc = bacc.Bacc("TRN2", target_bir_lowering=False, num_devices=1)
    args = [nc.dram_tensor(k, arrays[k].shape, mybir.dt.from_np(arrays[k].dtype), kind="ExternalInput").ap()
            for k in _INS]
    out = nc.dram_tensor("out", (B, C, S), F32, kind="ExternalOutput").ap()
    build(nc, *args, out)
    r = run_bass_kernel_spmd(nc, [arrays], core_ids=[0])
    return r.results[0]["out"].reshape(B, C, HW, HW)
```

```python
from contextlib import ExitStack

import concourse.bass as bass
from concourse import mybir

F32 = mybir.dt.float32
F16 = mybir.dt.float16
I32 = mybir.dt.int32
ALU = mybir.AluOpType
ACT = mybir.ActivationFunctionType
AX = mybir.AxisListType

P = 128
B, C, HW = 8, 512, 32
S = HW * HW
NC = C // P
HALF = 512
TOK = 128
D = 64
SEG = C // D
HPI = S // TOK
HPH = HALF // TOK
GRP = 16
WSCALE = 256.0
EPS = 1e-5
ROUND = 12582912.0
MAGIC = float(0x5F3759DF)
UNITS = SEG
MAX_QUOTA = [3, 3, 3, 3, 3, 1, 0, 0]

C_ID, C_GRP, C_ONE, C_IOTA, C_POS, C_END = 0, 128, 256, 320, 352, 384
B_Q, B_K, B_CONV, B_MASKW, B_FILT = 0, 4, 8, 12, 16


class Count:

    def __init__(self, per):
        self.n, self.per, self.i, self.entry = 0, per, None, 0

    def loop(self, i):
        self.i, self.entry = i, self.n

    def done(self, passes):
        assert self.n - self.entry == self.per, (self.n - self.entry, self.per)
        self.i, self.n = None, self.entry + self.per * passes

    def value(self):
        return self.n if self.i is None else self.i * self.per + self.n


def ring_items(u, nxt, prev, v_units, stat):
    first = sum(MAX_QUOTA[:u])
    tiles = [("max", first + k) for k in range(MAX_QUOTA[u])] if nxt else []
    at = {"a": tiles[0:1], "b": tiles[1:2], "c": tiles[2:]}
    at["d"] = [("value", u // 2)] if v_units and u % 2 else []
    if stat and u in (5, 7):
        at["d"].append(("stat", (u - 5) // 2))
    if nxt and u == 6:
        at["d"].append(("shift", 0))
    if prev and u == 1:
        at["d"].append(("den", 0))
    return at


def build(nc, x, wqT, wkT, wvT, chan, bv, wc, const, out):
    x_img = x.rearrange("b (c p) s -> b p c s", p=P)
    out_img = out.rearrange("b (c p) s -> b p c s", p=P)
    x1 = nc.dram_tensor("x1_scratch", (B, C, S), F32, kind="Internal").ap()
    x1_img = x1.rearrange("b (c p) s -> b p c s", p=P)

    top = ExitStack()
    with top:
        def sem(name):
            return top.enter_context(nc.semaphore(name))

        def sb(stack, name, shape, dt):
            return stack.enter_context(nc.sbuf_tensor(name, shape, dt))

        cst = sb(top, "cst", [P, C_END], F32)
        prm = sb(top, "prm", [P, 20], F32)
        bn = sb(top, "bn", [P, NC, 2, 6], F32)
        mv = sb(top, "mv", [P, NC, 2], F32)
        gmv = sb(top, "gmv", [P, NC, 2], F32)
        dm = sb(top, "dm", [P, NC], F32)
        ve = sb(top, "ve", [P, NC], F32)
        nt = sb(top, "nt", [P, 2, NC], F32)
        rstd = sb(top, "rstd", [P, NC], F32)
        nbias = sb(top, "nbias", [P, NC], F32)
        ident = cst[:, C_ID:C_ID + P]
        grp = cst[:, C_GRP:C_GRP + P]
        ones = cst[:, C_ONE:C_ONE + D]

        bank = [top.enter_context(nc.psum_tensor(f"bank{k}", [P, 512], F32)) for k in range(8)]
        sc_bank = bank[0:4]
        v_ring = bank[4:6]
        pv_bank = bank[6]
        qk_bank = bank[7]

        s_const = sem("const_loaded")
        s_stat = sem("stat_step")
        s_passed = sem("passed")
        s1 = {n: sem(n) for n in (
            "w_loaded0", "w_loaded1", "w_hi_done", "w_split", "x_loaded", "xr_loaded0", "xr_loaded1", "kb_clear", "xn_ready", "xn_hi", "xn_split",
            "qk_ready", "qk_out", "qk_hi", "qk_split", "qk_moved", "ring_full", "ring_free",
            "min_done", "shift_sent", "shift_row", "scores_full", "exp_done", "pv_done", "sum0", "sum1",
            "recip_done", "o_done", "resid_done", "x1_stored", "value_out")}

        def statistics(dve, xin, step):
            def chain(ins):
                ins.then_inc(s_stat, 1)
                step.n += 1

            def sync():
                dve.wait_ge(s_stat, step.value())

            def moments(c):
                for k in range(2):
                    chain(dve.bn_stats(bn[:, c, k], xin[:, c, k * 512:(k + 1) * 512]))

            def aggregate():
                sync()
                dve.sem_inc(s_passed, 1)
                for c in range(NC):
                    chain(dve.bn_aggr(mv[:, c], bn[:, c]))

            def centre(src):
                chain(dve.tensor_copy(gmv[:].rearrange("p c k -> p (c k)"), src[:, 0:2 * NC]))
                sync()
                chain(dve.tensor_tensor(dm[:], mv[:, :, 0], gmv[:, :, 0], ALU.subtract))
                sync()
                chain(dve.tensor_tensor(dm[:], dm[:], dm[:], ALU.mult))

            def finish(src):
                chain(dve.scalar_tensor_tensor(out=ve[:], in0=src[:, 0:NC], scalar=EPS, in1=gmv[:, :, 1],
                                               op0=ALU.add, op1=ALU.add))
                sync()
                chain(dve.tensor_scalar(nt[:, 0].bitcast(I32), ve[:].bitcast(I32), 1, None,
                                        ALU.logical_shift_right))
                sync()
                chain(dve.tensor_scalar(rstd[:].bitcast(I32), nt[:, 0].bitcast(I32), -1.0, MAGIC,
                                        ALU.mult, ALU.add))
                for _ in range(4):
                    sync()
                    chain(dve.tensor_tensor(nt[:, 0], rstd[:], rstd[:], ALU.mult))
                    sync()
                    chain(dve.scalar_tensor_tensor(out=nt[:, 1], in0=nt[:, 0], scalar=-0.5, in1=ve[:],
                                                   op0=ALU.mult, op1=ALU.mult))
                    sync()
                    chain(dve.scalar_tensor_tensor(out=rstd[:], in0=nt[:, 1], scalar=1.5, in1=rstd[:],
                                                   op0=ALU.add, op1=ALU.mult))
                sync()
                chain(dve.scalar_tensor_tensor(out=nbias[:], in0=gmv[:, :, 0], scalar=-1.0, in1=rstd[:],
                                               op0=ALU.mult, op1=ALU.mult))
            return moments, aggregate, centre, finish

        STAT_STEPS = 2 * NC + NC + 3 + 3 + 12 + 1
        STAT_AGG = 3 * NC
        STAT_DEV = STAT_AGG + 3

        def statistics_sum(pe, dst, k):
            if k == 0:
                return pe.matmul(dst[:, 0:2 * NC], grp, mv[:].rearrange("p c k -> p (c k)"),
                                 start=True, stop=True)
            return pe.matmul(dst[:, 0:NC], grp, dm[:], start=True, stop=True)

        st1 = ExitStack()
        w_hi = sb(st1, "w_hi", [P, 3, NC, C], F16)
        w_lo = sb(st1, "w_lo", [P, 3, NC, C], F16)
        bv_row = sb(st1, "bv_row", [P, C], F32)
        xs = sb(st1, "xs", [P, NC, S], F32)
        xr = sb(st1, "xr", [P, 2, NC, HALF], F32)
        xn32 = sb(st1, "xn32", [P, 2, HALF], F32)
        xn_hi = sb(st1, "xn_hi", [P, 2, NC, HALF], F16)
        xn_lo = sb(st1, "xn_lo", [P, 2, NC, HALF], F16)
        qk32 = sb(st1, "qk32", [P, 2, HALF], F32)
        qk_hi = sb(st1, "qk_hi", [P, 2, NC, HALF], F16)
        qk_lo = sb(st1, "qk_lo", [P, 2, NC, HALF], F16)
        k_a = sb(st1, "k_a", [P, 2, SEG, HALF], F16)
        q_a = sb(st1, "q_a", [P, 2, SEG, HALF], F16)
        k_b = sb(st1, "k_b", [P, 2, SEG, HALF], F16)
        q_b = sb(st1, "q_b", [P, 2, SEG, HALF], F16)
        val = sb(st1, "val", [P, 2, HPH, C], F32)
        prob = sb(st1, "prob", [P, 8, 512], F32)
        psum_acc = sb(st1, "prob_sum", [P, 2, 2, 512], F32)
        nmax = sb(st1, "nmax", [P, SEG, 2], F32)
        nmin = sb(st1, "nmin", [P, SEG], F32)
        shift = sb(st1, "shift", [SEG, 2, TOK], F16)
        o_sb = sb(st1, "o_sb", [P, 512], F32)
        q_av = q_a[:].rearrange("p h (j e) t -> p h e j t", e=2)
        q_bv = q_b[:].rearrange("p h (j e) t -> p h e j t", e=2)
        stage = prob[:].rearrange("p (a k) n -> p a k n", a=2)

        PER_RING = HPI * (16 + 1 + 1) + 2 * HPH + 2

        def tokens(s):
            return s // HPH, slice((s % HPH) * TOK, (s % HPH + 1) * TOK)

        st1.close()
        st2 = top.enter_context(ExitStack())
        PW = HW + 2
        PAIR = HW // 2
        u_hi = sb(st2, "u_hi", [P, 4, 3, NC, C], F16)
        u_lo = sb(st2, "u_lo", [P, 4, 3, NC, C], F16)
        xo = sb(st2, "xo", [P, 2, NC, S], F32)
        r_pad = sb(st2, "r_pad", [P, NC, PW, PW], F32)
        v_hi = sb(st2, "v_hi", [P, 4, NC, PW, PAIR], F16)
        v_lo = sb(st2, "v_lo", [P, 4, NC, PW, PAIR], F16)
        v32 = sb(st2, "v32", [P, NC * PW * PAIR], F32)
        g_mid = sb(st2, "g_mid", [P, NC, C], F32)
        rows = sb(st2, "rows", [P, NC, HW], F32)
        cols = sb(st2, "cols", [P, NC, HW], F32)
        wrow = sb(st2, "wrow", [P, NC, HW], F32)
        wcol = sb(st2, "wcol", [P, NC, HW], F32)
        mxy = sb(st2, "mxy", [P, 4, NC], F32)
        mwf = sb(st2, "mwf", [P, NC], F32)
        g_row = [xo[:, 1, 0:2].rearrange("p a (b n) -> p (a b) n", n=C), g_mid[:],
                 xo[:, 1, 2:4].rearrange("p a (b n) -> p (a b) n", n=C)]
        v32_v = v32[:].rearrange("p (c h w) -> p c h w", c=NC, w=PAIR)
        mask_v = v32[:, 0:2 * S].rearrange("p (a h w) -> p a h w", a=2, w=HW)
        xo_pair = xo[:].rearrange("p b c (n two) -> p b c n two", two=2)
        s2 = {n: sem(n) for n in (
            "g_loaded0", "g_loaded1", "g_loaded2", "g_mixed", "u_cast", "u_split", "pad_clear", "x_in0", "x_in1",
            "sum2_full", "sum2_free", "mask_step", "tables", "r_normed", "bias_in", "mask_out", "mask_used",
            "relu_done", "v_made", "v_cast", "v_split", "conv_full", "conv_free", "y_stored0", "y_stored1")}
        MASK_STEPS = 2 * NC + 3 + 3 + 1 + 2 + 3 + 6 + 1
        U_ORDER = (0, 3, 2, 1)
        GROUPS = 4 * NC
        READS = (1, 2, 2, 1)
        IMG_READS = NC * sum(READS)

        def reads_to(pos, co):
            if pos < 0:
                return co + 1
            return 4 + NC * sum(READS[:pos]) + READS[pos] * (co + 1)

        block = top.enter_context(nc.Block())

        @block.sync
        def _(sp):
            sp.dma_start(cst[:], const).then_inc(s_const, 16)
            sp.dma_start(prm[:], chan).then_inc(s_const, 16)
            sp.dma_start(bv_row[:], bv.partition_broadcast(P)).then_inc(s_const, 16)
            sp.dma_start(xs[:], x_img[0]).then_inc(s1["x_loaded"], 16)
            for k, w in enumerate((wqT, wkT, wvT)):
                if k == 2:
                    sp.wait_ge(s1["w_split"], 1)
                sp.dma_start(stage[:, k % 2], w.rearrange("(c p) n -> p c n", p=P)).then_inc(s1[f"w_loaded{k % 2}"], 16)
            sp.dma_start(xr[:, 0], x_img[0][:, :, 0:HALF]).then_inc(s1["xr_loaded0"], 16)

            def move_qk(which, t, half, first=False):
                sp.wait_ge(s1["qk_split"], 2 + 8 * t + 4 * (which + 1))
                if not first:
                    sp.sem_inc(s_passed, 1)
                    sp.wait_ge(s1["exp_done"], 4 + 64 * (t - 1))
                hi_to = ((k_a, 0), (k_b, 0)) if which == 0 else ((q_a, 0), (q_a, D))
                lo_to = (k_a, D) if which == 0 else (q_b, 0)
                for e in range(2):
                    src = slice(e * D, (e + 1) * D)
                    for dst, p0 in hi_to:
                        sp.dma_start(dst[p0:p0 + D, half, e::2, :], qk_hi[src, which]).then_inc(s1["qk_moved"], 16)
                    dst, p0 = lo_to
                    sp.dma_start(dst[p0:p0 + D, half, e::2, :], qk_lo[src, which]).then_inc(s1["qk_moved"], 16)

            def send_shift(h, s):
                half, tok = tokens(s)
                sp.wait_ge(s1["shift_sent"], h + 1)
                sp.dma_start(q_b[D:D + 1, half, :, tok], shift[:, s % 2]).then_inc(s1["shift_row"], 16)

            def store_x1(t, img, half):
                sp.wait_ge(s1["resid_done"], 1 + 4 * (t + 1))
                sp.sem_inc(s_passed, 1)
                sp.dma_start(x1_img[img][:, :, half * HALF:(half + 1) * HALF], xr[:, half]).then_inc(s1["x1_stored"], 16)

            def slot(img, s, prev=True, nxt=True, more=True):
                t = img * 2 + s // HPH
                r = s % HPH
                if r == 1 and (s < HPH or more):
                    move_qk(0, t + 1, 1 - s // HPH)
                if r == 2 and (s < HPH or more):
                    move_qk(1, t + 1, 1 - s // HPH)
                if r == 1 and (s < HPH or more):
                    sp.wait_ge(s1["x1_stored"], 16 + 16 * t)
                    if s < HPH:
                        src = x_img[img][:, :, HALF:S]
                    else:
                        src = x_img[img + 1][:, :, 0:HALF]
                    sp.dma_start(xr[:, 1 - s // HPH], src).then_inc(s1[f"xr_loaded{1 - s // HPH}"], 16)
                if s == 1 and more:
                    sp.wait_ge(s1["xn_ready"], 8 * (img + 1))
                    sp.dma_start(xs[:], x_img[img + 1]).then_inc(s1["x_loaded"], 16)
                if nxt:
                    send_shift(img * HPI + s + 1, (s + 1) % HPI)
                if r == 0 and prev:
                    if s == 0:
                        store_x1(t - 1, img - 1, 1)
                    else:
                        store_x1(t - 1, img, 0)

            sp.sem_inc(s1["x1_stored"], 16)
            sp.wait_ge(s1["kb_clear"], 6)
            move_qk(0, 0, 0, first=True)
            move_qk(1, 0, 0, first=True)
            send_shift(0, 0)
            slot(0, 0, prev=False)
            with sp.Fori(0, B - 1) as i:
                for s in range(1, HPI):
                    slot(i, s)
                slot(i + 1, 0)
            for s in range(1, HPI):
                slot(B - 1, s, nxt=s < HPI - 1, more=False)
            store_x1(2 * B - 1, B - 1, 1)
            sp.wait_ge(s1["x1_stored"], 16 + 16 * 2 * B)

            sp.dma_start(xo[:, 0], x1_img[0]).then_inc(s2["x_in0"], 16)
            for ky in range(3):
                for kx in (0, 2, 1):
                    if ky > 0:
                        if kx == 1:
                            sp.wait_ge(s2["g_mixed"], 3 * ky)
                        else:
                            sp.wait_ge(s2["u_split"], 4 * ky)
                            sp.wait_ge(s2["u_cast"], 4 * ky)
                    sp.dma_start(g_row[kx], wc[3 * ky + kx].rearrange("(c p) n -> p c n", p=P))\
                        .then_inc(s2[f"g_loaded{kx}"], 16)
            sp.wait_ge(s2["u_split"], 12)
            sp.wait_ge(s2["g_mixed"], 9)
            sp.dma_start(xo[:, 1], x1_img[1]).then_inc(s2["x_in1"], 16)

            def store_image(img, b, load):
                for co in range(NC):
                    sp.wait_ge(s2["conv_free"], IMG_READS * img + reads_to(3, co))
                    sp.dma_start(out_img[img][:, co], xo[:, b, co]).then_inc(s2[f"y_stored{b}"], 16)
                if load is not None:
                    sp.wait_ge(s2[f"y_stored{b}"], 16 * NC * load)
                    sp.dma_start(xo[:, b], x1_img[img + 2]).then_inc(s2[f"x_in{b}"], 16)

            with sp.Fori(0, B // 2 - 1) as j:
                for b in range(2):
                    store_image(j * 2 + b, b, j + 1)
            for b in range(2):
                store_image(B - 2 + b, b, None)
            for b in range(2):
                sp.wait_ge(s2[f"y_stored{b}"], 16 * NC * (B // 2))

        @block.tensor
        def _(pe):
            ring = Count(PER_RING)

            def take():
                pe.wait_ge(s1["ring_free"], ring.value() + 1)
                dst = v_ring[ring.n % 2]
                ring.n += 1
                return dst

            def stat_item(img, k):
                dst = take()
                pe.wait_ge(s_stat, img * STAT_STEPS + (STAT_AGG, STAT_DEV)[k])
                statistics_sum(pe, dst, k).then_inc(s1["ring_full"], 1)

            def project_qk(t, half, which, j):
                w = 1 - which
                pe.wait_ge(s1["xn_split"], 2 + 4 * (t + 1))
                pe.wait_ge(s1["qk_out"], 8 * t + 4 * which + j + 1)
                steps = [(a, b, c) for c in range(NC) for a, b in
                         ((w_hi, xn_hi), (w_hi, xn_lo), (w_lo, xn_hi))]
                for n, (a, b, c) in enumerate(steps):
                    mm = pe.matmul(qk_bank[:], a[:, w, c, j * P:(j + 1) * P], b[:, half, c],
                                   start=(n == 0), stop=(n == len(steps) - 1))
                mm.then_inc(s1["qk_ready"], 1)

            def project_value(t, half, g):
                pe.wait_ge(s1["xn_split"], 2 + 4 * (t + 1))
                dst = take()
                steps = [(a, b, c) for c in range(NC) for a, b in
                         ((xn_hi, w_hi), (xn_hi, w_lo), (xn_lo, w_hi))]
                for n, (a, b, c) in enumerate(steps):
                    mm = pe.matmul(dst[:], a[:, half, c, g * TOK:(g + 1) * TOK], b[:, 2, c],
                                   start=(n == 0), stop=(n == len(steps) - 1))
                mm.then_inc(s1["ring_full"], 1)

            def max_tile(s, m):
                half, tok = tokens(s)
                dst = take()
                pe.matmul(dst[:].rearrange("p (k t) -> p k t", t=TOK), q_a[:, half, m // 2, tok],
                          k_a[:, half, 4 * (m % 2):4 * (m % 2) + 4, tok],
                          start=True, stop=True).then_inc(s1["ring_full"], 1)

            def shift_item(h):
                dst = take()
                pe.wait_ge(s1["min_done"], h + 1)
                pe.matmul(dst[0:SEG, 0:TOK], nmin[:], ident, start=True, stop=True).then_inc(s1["ring_full"], 1)

            def den_item(h, par):
                dst = take()
                pe.wait_ge(s1["sum0"], 7 + 7 * (h + 1))
                pe.matmul(dst[0:D, :], ones, psum_acc[:, par, 0], start=True, stop=True)
                pe.wait_ge(s1["sum1"], 7 + 7 * (h + 1))
                pe.matmul(dst[D:P, :], ones, psum_acc[:, par, 1], start=True, stop=True).then_inc(s1["ring_full"], 1)

            def scores(h, s, u, part):
                half, tok = tokens(s)
                k_op, q_op = ((k_a, q_av), (k_b, q_bv))[part]
                for e in range(2):
                    b = (s * 16 + u * 2 + e) % 4
                    if part == 0:
                        pe.wait_ge(s1["exp_done"], 16 * h + 2 * u + e + 1)
                    mm = pe.matmul(sc_bank[b][:].rearrange("p (j t) -> p j t", t=TOK), k_op[:, half, u, tok],
                                   q_op[:, half, e, :, tok], start=(part == 0), stop=(part == 1))
                    if part == 1:
                        mm.then_inc(s1["scores_full"], 1)

            def weigh(h, s, kc):
                if kc == 0:
                    pe.wait_ge(s1["o_done"], h + 1)
                    pe.wait_ge(s1["value_out"], h + 1)
                for e in range(2):
                    pe.wait_ge(s1["exp_done"], 4 + 16 * h + 2 * kc + e + 1)
                    pe.matmul(pv_bank[e * D:(e + 1) * D, :], val[:, s // HPH, s % HPH, kc * D:(kc + 1) * D],
                              prob[:, (2 * kc + e) % 8], start=(kc == 0),
                              stop=(kc == SEG - 1)).then_inc(s1["pv_done"], 1)

            def slot(img, s, prev=True, nxt=True, more=True):
                h = img * HPI + s
                t = img * 2 + s // HPH
                r = s % HPH
                proj = r < 3 and (s < HPH or more)
                for u in range(UNITS):
                    items = ring_items(u, nxt, prev, proj and r == 2, s == 2 and more)

                    def run(place):
                        for kind, a in items[place]:
                            if kind == "max":
                                max_tile((s + 1) % HPI, a)
                            elif kind == "value":
                                project_value(t + 1, 1 - s // HPH, a)
                            elif kind == "stat":
                                stat_item(img + 1, a)
                            elif kind == "shift":
                                shift_item(h + 1)
                            else:
                                den_item(h - 1, (s - 1) % 2)
                    if u == 0 and nxt and r == 3:
                        pe.wait_ge(s1["qk_moved"], 192 * (t + 2))
                    run("a")
                    scores(h, s, u, 0)
                    run("b")
                    if u == 0:
                        pe.wait_ge(s1["shift_row"], 16 * (h + 1))
                    scores(h, s, u, 1)
                    run("c")
                    if proj and r < 2 and u % 2:
                        project_qk(t + 1, 1 - s // HPH, r, u // 2)
                    run("d")
                    if u == 0 and prev:
                        weigh(h - 1, (s - 1) % HPI, SEG - 1)
                    if u == 2:
                        weigh(h, s, 0)
                    if u >= 2:
                        weigh(h, s, u - 1)

            pe.sem_inc(s1["pv_done"], 8)
            pe.wait_ge(s_const, 48)
            stat_item(0, 0)
            stat_item(0, 1)
            pe.wait_ge(s1["w_split"], 3)
            for which in range(2):
                for j in range(NC):
                    project_qk(0, 0, which, j)
            for g in range(HPH):
                project_value(0, 0, g)
            pe.wait_ge(s1["qk_moved"], 192)
            for m in range(16):
                max_tile(0, m)
            shift_item(0)
            slot(0, 0, prev=False)
            with pe.Fori(0, B - 1) as i:
                ring.loop(i)
                for s in range(1, HPI):
                    slot(i, s)
                slot(i + 1, 0)
            ring.done(B - 1)
            for s in range(1, HPI):
                slot(B - 1, s, nxt=s < HPI - 1, more=False)
            weigh(B * HPI - 1, HPI - 1, SEG - 1)
            den_item(B * HPI - 1, 1)

            pe.wait_ge(s1["o_done"], B * HPI + 1)
            pe.sem_inc(s2["conv_full"], GROUPS)

            def stat2(img, k):
                pe.wait_ge(s2["sum2_free"], img * 2 + k + 1)
                pe.wait_ge(s_stat, STAT_STEPS * B + img * STAT_STEPS + (STAT_AGG, STAT_DEV)[k])
                statistics_sum(pe, qk_bank, k).then_inc(s2["sum2_full"], 1)

            def convolve(img, more=True):
                for pos in range(4):
                    pe.wait_ge(s2["u_split"], 9 if pos == 0 else 12)
                    pe.wait_ge(s2["v_split"], img * 4 + pos + 2)
                    for co in range(NC):
                        pe.wait_ge(s2["conv_free"], IMG_READS * img + reads_to(pos - 1, co))
                        steps = [(ky, c, u, v) for ky in range(3) for c in range(NC) for u, v in
                                 ((u_hi, v_hi), (u_hi, v_lo), (u_lo, v_hi))]
                        for n, (ky, c, u, v) in enumerate(steps):
                            mm = pe.matmul(bank[co][:].rearrange("p (h w) -> p h w", w=PAIR),
                                           u[:, pos, ky, c, co * P:(co + 1) * P],
                                           v[:, pos, c, ky:ky + HW, :],
                                           start=(n == 0), stop=(n == len(steps) - 1))
                        mm.then_inc(s2["conv_full"], 1)
                        if more and pos * NC + co in (3, 4):
                            stat2(img + 1, pos * NC + co - 3)

            stat2(0, 0)
            stat2(0, 1)
            with pe.Fori(0, B - 1) as i:
                convolve(i)
            convolve(B - 1, more=False)

        @block.scalar
        def _(act):
            def normed(img, half, c):
                k = 4 * half + c
                act.wait_ge(s_stat, (img + 1) * STAT_STEPS)
                act.wait_ge(s1["xn_split"], img * 8 + k + 1)
                act.activation(xn32[:, c % 2], xs[:, c, half * HALF:(half + 1) * HALF], ACT.Identity,
                               bias=nbias[:, c:c + 1], scale=rstd[:, c:c + 1]).then_inc(s1["xn_ready"], 1)

            def qk_evacuate(t, which, j):
                act.wait_ge(s1["qk_ready"], 8 * t + 4 * which + j + 1)
                act.wait_ge(s1["qk_split"], 8 * t + 4 * which + j + 1)
                col = (B_K, B_Q)[which] + j
                act.activation(qk32[:, j % 2], qk_bank[:], ACT.Identity, bias=prm[:, col:col + 1],
                               scale=1.0 / WSCALE).then_inc(s1["qk_out"], 1)

            def exp_tile(h, u, e):
                act.wait_ge(s1["scores_full"], 16 * h + 2 * u + e + 1)
                act.wait_ge(s1["pv_done"], 16 * h + 2 * u + e + 1)
                act.wait_ge(s1[f"sum{e}"], 7 * h + (u + 4 if u < 4 else 7 + max(u - 4, 1)))
                act.activation(prob[:, (2 * u + e) % 8], sc_bank[(2 * u + e) % 4][:], ACT.Exp,
                               scale=float(D) ** -0.5).then_inc(s1["exp_done"], 1)

            def slot(img, s, more=True):
                h = img * HPI + s
                t = img * 2 + s // HPH
                r = s % HPH
                for u in range(UNITS):
                    exp_tile(h, u, 0)
                    exp_tile(h, u, 1)
                    if r < 2 and u % 2 and (s < HPH or more):
                        qk_evacuate(t + 1, r, u // 2)
                    if s == 3 and more and 1 <= u < 5:
                        normed(img + 1, 0, u - 1)
                    if s == 4 and more and u < 4:
                        normed(img + 1, 1, u)

            act.sem_inc(s1["exp_done"], 4)
            act.sem_inc(s1["qk_out"], 1)
            act.wait_ge(s_const, 48)
            for half in range(2):
                for c in range(NC):
                    normed(0, half, c)
            for which in range(2):
                for j in range(NC):
                    qk_evacuate(0, which, j)
            slot(0, 0)
            with act.Fori(0, B - 1) as i:
                for s in range(1, HPI):
                    slot(i, s)
                slot(i + 1, 0)
            for s in range(1, HPI):
                slot(B - 1, s, more=False)

            act.wait_ge(s1["x1_stored"], 16 + 16 * 2 * B)

            def cast_filters(ky):
                for k, pos in enumerate(U_ORDER):
                    if pos in (0, 3):
                        act.wait_ge(s2[f"g_loaded{0 if pos == 0 else 2}"], 16 * (ky + 1))
                    else:
                        act.wait_ge(s2["g_mixed"], 3 * ky + k)
                    act.activation(u_hi[:, pos, ky], g_row[2 if pos in (2, 3) else 0], ACT.Copy,
                                   scale=WSCALE if pos in (0, 3) else WSCALE / 2).then_inc(s2["u_cast"], 1)

            def norm_image(img, b):
                act.wait_ge(s_stat, STAT_STEPS * B + (img + 1) * STAT_STEPS)
                act.wait_ge(s2["v_made"], 4 * img + 1)
                for c in range(NC):
                    act.activation(r_pad[:, c, 1:HW + 1, 1:HW + 1], xo[:, b, c].rearrange("p (h w) -> p h w", w=HW),
                                   ACT.Identity, bias=nbias[:, c:c + 1], scale=rstd[:, c:c + 1])\
                        .then_inc(s2["r_normed"], 1)
                act.wait_ge(s2["r_normed"], 4 * img + 4)
                act.sem_inc(s_passed, 1)
                for c in range(NC):
                    act.activation(xo[:, b, c], xo[:, b, c], ACT.Identity, bias=prm[:, B_CONV + c:B_CONV + c + 1],
                                   scale=1.0).then_inc(s2["bias_in"], 1)

            def relu(img, c):
                act.wait_ge(s2["mask_used"], 4 * img + c + 1)
                act.activation(r_pad[:, c, 1:HW + 1, 1:HW + 1], r_pad[:, c, 1:HW + 1, 1:HW + 1], ACT.Relu)\
                    .then_inc(s2["relu_done"], 1)

            def cast_v(img, pos):
                act.wait_ge(s2["v_made"], 4 * img + pos + 2)
                act.wait_ge(s2["conv_full"], GROUPS * img + NC * (pos + 1))
                act.activation(v_hi[:, pos], v32_v, ACT.Copy).then_inc(s2["v_cast"], 1)

            def prepare(img, b):
                norm_image(img, b)
                for c in range(NC):
                    relu(img, c)
                for pos in range(3):
                    cast_v(img, pos)

            cast_filters(0)
            norm_image(0, 0)
            cast_filters(1)
            for c in range(NC):
                relu(0, c)
            cast_v(0, 0)
            cast_filters(2)
            cast_v(0, 1)
            cast_v(0, 2)
            with act.Fori(0, B // 2 - 1) as j:
                for b in range(2):
                    cast_v(j * 2 + b, 3)
                    prepare(j * 2 + b + 1, 1 - b)
            cast_v(B - 2, 3)
            prepare(B - 1, 1)
            cast_v(B - 1, 3)

        @block.gpsimd
        def _(pool):
            def add_tile(h, s, kc):
                pool.wait_ge(s1["exp_done"], 4 + 16 * h + 2 * kc + 2)
                acc = psum_acc[:, s % 2, 1]
                pool.wait_ge(s1["sum1"], 7 + 7 * h + kc - 1)
                in0 = prob[:, 1] if kc == 1 else acc
                nc.gpsimd.tensor_tensor(acc, in0, prob[:, (2 * kc + 1) % 8], ALU.add).then_inc(s1["sum1"], 1)

            def residual(h, s):
                half, tok = tokens(s)
                pool.wait_ge(s1["o_done"], 1 + h + 1)
                o_v = o_sb[:].rearrange("p (j t) -> p j t", t=TOK)
                nc.gpsimd.tensor_tensor(xr[:, half, :, tok], xr[:, half, :, tok], o_v, ALU.add)\
                    .then_inc(s1["resid_done"], 1)

            def slot(img, s, prev=True):
                h = img * HPI + s
                for u in range(UNITS):
                    if u == 0 and prev:
                        add_tile(h - 1, (s - 1) % HPI, SEG - 1)
                    if u >= 2:
                        add_tile(h, s, u - 1)
                    if u == 2 and prev:
                        if s % HPH == 1:
                            pool.wait_ge(s1[f"xr_loaded{s // HPH}"], 16 * (img + 1))
                        residual(h - 1, (s - 1) % HPI)

            nc.gpsimd.memset(k_b[D:P], 0.0).then_inc(s1["kb_clear"], 1)
            nc.gpsimd.memset(q_b[D:P], 0.0).then_inc(s1["kb_clear"], 1)
            pool.wait_ge(s1["kb_clear"], 2)
            nc.gpsimd.memset(k_b[D:D + 1], 8.0).then_inc(s1["kb_clear"], 4)
            pool.sem_inc(s1["sum1"], 7)
            pool.sem_inc(s1["resid_done"], 1)
            slot(0, 0, prev=False)
            with pool.Fori(0, B - 1) as i:
                for s in range(1, HPI):
                    slot(i, s)
                slot(i + 1, 0)
            for s in range(1, HPI):
                slot(B - 1, s)
            add_tile(B * HPI - 1, HPI - 1, SEG - 1)
            residual(B * HPI - 1, HPI - 1)

            pool.wait_ge(s1["x1_stored"], 16 + 16 * 2 * B)
            nc.gpsimd.memset(r_pad[:], 0.0).then_inc(s2["pad_clear"], 1)

            def mix_filters(ky):
                pool.wait_ge(s2["g_loaded2"], 16 * (ky + 1))
                pool.wait_ge(s2["u_split"], 4 * ky + 1)
                nc.gpsimd.tensor_tensor(g_row[0], g_row[0], g_row[2], ALU.add).then_inc(s2["g_mixed"], 1)
                pool.wait_ge(s2["g_loaded1"], 16 * (ky + 1))
                pool.wait_ge(s2["u_split"], 4 * ky + 2)
                pool.wait_ge(s2["g_mixed"], 3 * ky + 1)
                nc.gpsimd.tensor_tensor(g_row[2], g_row[0], g_row[1], ALU.subtract).then_inc(s2["g_mixed"], 1)
                pool.wait_ge(s2["g_mixed"], 3 * ky + 2)
                nc.gpsimd.tensor_tensor(g_row[0], g_row[0], g_row[1], ALU.add).then_inc(s2["g_mixed"], 1)

            def mask_image(img):
                pool.wait_ge(s2["tables"], img + 1)
                pool.wait_ge(s2["v_split"], 4 * img + 1)
                for c in range(NC):
                    if c >= 2:
                        pool.wait_ge(s2["mask_used"], 4 * img + c - 1)
                    nc.gpsimd.tensor_tensor(mask_v[:, c % 2], wrow[:, c].unsqueeze(2).broadcast_to([P, HW, HW]),
                                            wcol[:, c].unsqueeze(1).broadcast_to([P, HW, HW]), ALU.subtract)\
                        .then_inc(s2["mask_out"], 1)

            mix_filters(0)
            mix_filters(1)
            mask_image(0)
            mix_filters(2)
            with pool.Fori(1, B) as i:
                mask_image(i)

        @block.vector
        def _(dve):
            ring = Count(PER_RING)
            step = Count(STAT_STEPS)

            def item():
                dve.wait_ge(s1["ring_full"], ring.value() + 1)
                src = v_ring[ring.n % 2]
                ring.n += 1
                return src

            moments, aggregate, centre, finish = statistics(dve, xs, step)

            def split_norm(img, half, c):
                k = 4 * half + c
                dve.wait_ge(s1["xn_ready"], img * 8 + k + 1)
                dve.tensor_copy(xn_hi[:, half, c], xn32[:, c % 2]).then_inc(s1["xn_hi"], 1)
                dve.wait_ge(s1["xn_hi"], img * 8 + k + 1)
                dve.tensor_tensor(xn_lo[:, half, c], xn32[:, c % 2], xn_hi[:, half, c], ALU.subtract)\
                    .then_inc(s1["xn_split"], 1)

            def split_qk(t, which, j):
                n = 8 * t + 4 * which + j
                dve.wait_ge(s1["qk_out"], 1 + n + 1)
                if j == 0:
                    dve.wait_ge(s1["qk_moved"], 192 * t)
                dve.tensor_copy(qk_hi[:, which, j], qk32[:, j % 2]).then_inc(s1["qk_hi"], 1)
                dve.wait_ge(s1["qk_hi"], n + 1)
                dve.tensor_tensor(qk_lo[:, which, j], qk32[:, j % 2], qk_hi[:, which, j], ALU.subtract)\
                    .then_inc(s1["qk_split"], 1)

            def add_tile(h, s, kc):
                dve.wait_ge(s1["exp_done"], 4 + 16 * h + 2 * kc + 1)
                acc = psum_acc[:, s % 2, 0]
                dve.wait_ge(s1["sum0"], 7 + 7 * h + kc - 1)
                in0 = prob[:, 0] if kc == 1 else acc
                dve.tensor_tensor(acc, in0, prob[:, (2 * kc) % 8], ALU.add).then_inc(s1["sum0"], 1)

            def max_item(h, m):
                src = item()
                if m == 0:
                    dve.wait_ge(s1["min_done"], h)
                dve.tensor_reduce(nmax[:, m // 2, m % 2:m % 2 + 1], src[:], AX.X, ALU.max, negate=True)\
                    .then_inc(s1["ring_free"], 1)
                if m == 15:
                    dve.wait_ge(s1["ring_free"], 2 + ring.value())
                    dve.tensor_tensor(nmin[:], nmax[:, :, 0], nmax[:, :, 1], ALU.min).then_inc(s1["min_done"], 1)

            def shift_item(h, s):
                src = item()
                if s > 0:
                    dve.wait_ge(s1["shift_row"], 16 * (h - 1))
                dve.tensor_scalar(shift[:, s % 2], src[0:SEG, 0:TOK], 0.125, None, ALU.mult)\
                    .then_inc(s1["shift_sent"], 1)
                dve.wait_ge(s1["shift_sent"], h + 1)
                dve.sem_inc(s1["ring_free"], 1)

            def value_item(h, half, g):
                src = item()
                dve.scalar_tensor_tensor(out=val[:, half, g], in0=src[:], scalar=1.0 / WSCALE, in1=bv_row[:],
                                         op0=ALU.mult, op1=ALU.add).then_inc(s1["value_out"], 1)
                dve.wait_ge(s1["value_out"], h + 1)
                dve.sem_inc(s1["ring_free"], 1)

            def den_item(h, s):
                src = item()
                dve.wait_ge(s1["resid_done"], h + 1)
                dve.reciprocal(o_sb[:], src[:]).then_inc(s1["ring_free"], 1)
                dve.wait_ge(s1["ring_free"], 2 + ring.value())
                dve.wait_ge(s1["pv_done"], 8 + 16 * (h + 1))
                dve.tensor_tensor(o_sb[:], pv_bank[:], o_sb[:], ALU.mult).then_inc(s1["o_done"], 1)

            def stat_item(img, k):
                src = item()
                (centre, finish)[k](src)
                dve.wait_ge(s_stat, step.value())
                dve.sem_inc(s1["ring_free"], 1)

            def slot(img, s, prev=True, nxt=True, more=True):
                h = img * HPI + s
                t = img * 2 + s // HPH
                r = s % HPH
                proj = r < 3 and (s < HPH or more)
                for u in range(UNITS):
                    if u == 0 and prev:
                        add_tile(h - 1, (s - 1) % HPI, SEG - 1)
                    if u >= 2:
                        add_tile(h, s, u - 1)
                    if s == 2 and more:
                        if u == 0:
                            dve.wait_ge(s1["x_loaded"], 16 * (img + 2))
                        if u < 4:
                            moments(u)
                        if u == 4:
                            aggregate()
                    items = ring_items(u, nxt, prev, proj and r == 2, s == 2 and more)
                    for place in "abcd":
                        for kind, a in items[place]:
                            if kind == "max":
                                max_item(h + 1, a)
                            elif kind == "value":
                                value_item(4 * (t + 1) + a, 1 - s // HPH, a)
                            elif kind == "stat":
                                stat_item(img + 1, a)
                            elif kind == "shift":
                                shift_item(h + 1, s + 1)
                            else:
                                den_item(h - 1, s - 1)
                    if s < HPH or more:
                        if r == 0 and u in (2, 4, 6):
                            split_qk(t + 1, 0, u // 2 - 1)
                        if r == 1:
                            if u == 0:
                                split_qk(t + 1, 0, 3)
                            if u in (2, 4, 6):
                                split_qk(t + 1, 1, u // 2 - 1)
                        if r == 2 and u == 0:
                            split_qk(t + 1, 1, 3)
                    if s == 3 and more and 2 <= u < 6:
                        split_norm(img + 1, 0, u - 2)
                    if s == 4 and more and 1 <= u < 5:
                        split_norm(img + 1, 1, u - 1)

            for name, credit in (("ring_free", 2), ("sum0", 7), ("o_done", 1), ("qk_split", 2), ("xn_split", 2)):
                dve.sem_inc(s1[name], credit)
            dve.wait_ge(s1["x_loaded"], 16)
            for c in range(NC):
                moments(c)
            aggregate()
            dve.wait_ge(s_const, 48)
            stat_item(0, 0)
            stat_item(0, 1)
            for k in range(3):
                dve.wait_ge(s1[f"w_loaded{k % 2}"], 16 * (k // 2 + 1))
                hi, lo = (t_[:, k].rearrange("p c n -> p (c n)") for t_ in (w_hi, w_lo))
                src = stage[:, k % 2].rearrange("p c n -> p (c n)")
                dve.tensor_scalar(hi, src, WSCALE, None, ALU.mult).then_inc(s1["w_hi_done"], 1)
                dve.wait_ge(s1["w_hi_done"], k + 1)
                dve.scalar_tensor_tensor(out=lo, in0=src, scalar=WSCALE, in1=hi,
                                         op0=ALU.mult, op1=ALU.subtract).then_inc(s1["w_split"], 1)
            for half in range(2):
                for c in range(NC):
                    split_norm(0, half, c)
            for which in range(2):
                for j in range(NC):
                    split_qk(0, which, j)
            for g in range(HPH):
                value_item(g, 0, g)
            for m in range(16):
                max_item(0, m)
            shift_item(0, 0)
            slot(0, 0, prev=False)
            with dve.Fori(0, B - 1) as i:
                ring.loop(i)
                step.loop(i)
                for s in range(1, HPI):
                    slot(i, s)
                slot(i + 1, 0)
            ring.done(B - 1)
            step.done(B - 1)
            for s in range(1, HPI):
                slot(B - 1, s, nxt=s < HPI - 1, more=False)
            add_tile(B * HPI - 1, HPI - 1, SEG - 1)
            den_item(B * HPI - 1, HPI - 1)

            dve.wait_ge(s1["x1_stored"], 16 + 16 * 2 * B)
            for name, credit in (("sum2_free", 1), ("v_made", 1), ("v_split", 1), ("conv_free", 4)):
                dve.sem_inc(s2[name], credit)
            mstep = Count(2 * MASK_STEPS)
            mstep.n = 0
            step.per = 2 * STAT_STEPS

            def chain(ins):
                ins.then_inc(s2["mask_step"], 1)
                mstep.n += 1

            def sync():
                dve.wait_ge(s2["mask_step"], mstep.value())

            iota = cst[:, C_IOTA:C_IOTA + HW].unsqueeze(1).broadcast_to([P, NC, HW])
            place = cst[:, C_POS:C_POS + HW].unsqueeze(1).broadcast_to([P, NC, HW])

            def over_hw(v):
                return v.unsqueeze(2).broadcast_to([P, NC, HW])

            def split_filters(ky):
                for k, pos in enumerate(U_ORDER):
                    dve.wait_ge(s2["u_cast"], 4 * ky + k + 1)
                    dve.scalar_tensor_tensor(out=u_lo[:, pos, ky], in0=g_row[2 if pos in (2, 3) else 0],
                                             scalar=WSCALE if pos in (0, 3) else WSCALE / 2,
                                             in1=u_hi[:, pos, ky], op0=ALU.mult, op1=ALU.subtract)\
                        .then_inc(s2["u_split"], 1)

            def moments2(img, b, loads):
                dve.wait_ge(s2[f"x_in{b}"], 16 * loads)
                moments, aggregate, _, _ = statistics(dve, xo[:, b], step)
                for c in range(NC):
                    moments(c)
                aggregate()

            def group_sum(img, k):
                dve.wait_ge(s2["sum2_full"], img * 2 + k + 1)
                (centre, finish)[k](qk_bank)
                dve.wait_ge(s_stat, step.value())
                dve.sem_inc(s2["sum2_free"], 1)

            def sums(img):
                dve.wait_ge(s2["r_normed"], 4 * img + 4)
                dve.sem_inc(s_passed, 1)
                for c in range(NC):
                    v = r_pad[:, c, 1:HW + 1, 1:HW + 1]
                    chain(dve.tensor_reduce(rows[:, c], v, AX.X, ALU.add))
                    chain(dve.tensor_reduce(cols[:, c], v.rearrange("p h w -> p w h"), AX.X, ALU.add))

            def make_tables():
                sync()
                chain(dve.tensor_tensor(wrow[:], rows[:], iota, ALU.mult))
                chain(dve.tensor_tensor(wcol[:], cols[:], iota, ALU.mult))
                chain(dve.tensor_reduce(mxy[:, 2], rows[:], AX.X, ALU.add))
                sync()
                chain(dve.tensor_reduce(mxy[:, 0], wrow[:], AX.X, ALU.add))
                chain(dve.tensor_reduce(mxy[:, 1], wcol[:], AX.X, ALU.add))
                chain(dve.tensor_scalar(mxy[:, 2], mxy[:, 2], 1e-9, None, ALU.max))
                sync()
                chain(dve.reciprocal(mxy[:, 3], mxy[:, 2]))
                sync()
                for a in range(2):
                    chain(dve.tensor_tensor(mxy[:, a], mxy[:, a], mxy[:, 3], ALU.mult))
                sync()
                chain(dve.tensor_scalar(mxy[:, 0:2], mxy[:, 0:2], 1.0, float(HW), ALU.max, ALU.min))
                sync()
                chain(dve.tensor_scalar(mxy[:, 0:2], mxy[:, 0:2], ROUND, ROUND, ALU.add, ALU.subtract))
                sync()
                chain(dve.tensor_scalar(mxy[:, 0:2], mxy[:, 0:2], 2.0 / (HW - 1), -1.0 - 2.0 / (HW - 1),
                                        ALU.mult, ALU.add))
                sync()
                for a, w in enumerate((wrow, wcol)):
                    chain(dve.tensor_tensor(w[:], place, over_hw(mxy[:, a]), ALU.subtract))
                sync()
                for w in (wrow, wcol):
                    chain(dve.scalar_tensor_tensor(out=w[:], in0=w[:], scalar=-1.0, in1=w[:],
                                                   op0=ALU.mult, op1=ALU.max))
                sync()
                for w in (wrow, wcol):
                    chain(dve.tensor_tensor(w[:], w[:], over_hw(mwf[:]), ALU.mult))
                sync()
                chain(dve.tensor_scalar(wrow[:], wrow[:], -1.0, 1.0, ALU.mult, ALU.add))
                sync()
                dve.sem_inc(s2["tables"], 1)

            def mask_chunk(img, c):
                dve.wait_ge(s2["mask_out"], 4 * img + c + 1)
                v = r_pad[:, c, 1:HW + 1, 1:HW + 1]
                dve.scalar_tensor_tensor(out=v, in0=mask_v[:, c % 2], scalar=-1.0, in1=v,
                                         op0=ALU.max, op1=ALU.mult).then_inc(s2["mask_used"], 1)

            def make_v(img, pos):
                if pos == 0:
                    dve.wait_ge(s2["relu_done"], 4 * img + 4)
                dve.wait_ge(s2["v_split"], 4 * img + pos + 1)
                a, b, op = ((0, 2, ALU.subtract), (1, 2, ALU.add), (2, 1, ALU.subtract), (1, 3, ALU.subtract))[pos]
                d = [r_pad[:, :, :, k:k + HW - 1:2] for k in range(4)]
                dve.tensor_tensor(v32_v, d[a], d[b], op).then_inc(s2["v_made"], 1)

            def split_v(img, pos):
                dve.wait_ge(s2["v_cast"], 4 * img + pos + 1)
                dve.tensor_tensor(v_lo[:, pos], v32_v, v_hi[:, pos], ALU.subtract).then_inc(s2["v_split"], 1)

            def add_group(img, b, n):
                pos, co = n // NC, n % NC
                dve.wait_ge(s2["conv_full"], GROUPS * (img + 1) + n + 1)
                if pos == 0 and co == 0:
                    dve.wait_ge(s2["bias_in"], 4 * img + 4)
                dve.wait_ge(s2["conv_free"], IMG_READS * img + reads_to(pos - 1, co))
                for odd, factor in (((0, 1),), ((0, 1), (1, 1)), ((0, 1), (1, -1)), ((1, -1),))[pos]:
                    y = xo_pair[:, b, co, :, odd]
                    dve.scalar_tensor_tensor(out=y, in0=bank[co][:], scalar=factor / WSCALE, in1=y,
                                             op0=ALU.mult, op1=ALU.add).then_inc(s2["conv_free"], 1)

            def image(img, b, loads=None):
                make_v(img, 3)
                add_group(img, b, 0)
                split_v(img, 3)
                for n in range(1, GROUPS):
                    add_group(img, b, n)
                    if loads is None:
                        continue
                    if n == 1:
                        moments2(img + 1, 1 - b, loads)
                    if n == 3:
                        group_sum(img + 1, 0)
                    if n == 4:
                        group_sum(img + 1, 1)
                    if n == 5:
                        sums(img + 1)
                    if n == 6:
                        make_tables()
                    if 7 <= n < 9:
                        mask_chunk(img + 1, 2 * n - 14)
                        mask_chunk(img + 1, 2 * n - 13)
                    if n >= 11 and n < 14:
                        split_v(img + 1, n - 11)
                    if n >= 10 and n < 13:
                        make_v(img + 1, n - 10)

            dve.tensor_scalar(mwf[:], prm[:, B_FILT:B_FILT + NC], 1.0, None, ALU.is_equal).then_inc(s_passed, 1)
            moments2(0, 0, 1)
            split_filters(0)
            group_sum(0, 0)
            group_sum(0, 1)
            dve.wait_ge(s2["pad_clear"], 1)
            dve.tensor_tensor(mwf[:], mwf[:], prm[:, B_MASKW:B_MASKW + NC], ALU.mult).then_inc(s2["pad_clear"], 1)
            dve.wait_ge(s2["pad_clear"], 2)
            sums(0)
            make_tables()
            split_filters(1)
            for c in range(NC):
                mask_chunk(0, c)
            make_v(0, 0)
            split_v(0, 0)
            split_filters(2)
            for pos in (1, 2):
                make_v(0, pos)
                split_v(0, pos)
            with dve.Fori(0, B // 2 - 1) as j:
                step.loop(j)
                mstep.loop(j)
                image(j * 2, 0, j + 1)
                image(j * 2 + 1, 1, j + 2)
            step.done(B // 2 - 1)
            mstep.done(B // 2 - 1)
            image(B - 2, 0, B // 2)
            image(B - 1, 1)


_INS = ["x", "wqT", "wkT", "wvT", "chan", "bv", "wc", "const"]


def constants(np):
    c = np.zeros((P, C_END), np.float32)
    c[:, C_ID:C_ID + P] = np.eye(P)
    c[:, C_GRP:C_GRP + P] = np.kron(np.eye(P // GRP), np.full((GRP, GRP), 1.0 / GRP))
    c[:, C_ONE:C_ONE + D] = 1.0
    c[:, C_IOTA:C_IOTA + HW] = np.arange(1, HW + 1)
    c[:, C_POS:C_POS + HW] = np.linspace(-1.0, 1.0, HW)
    return c


def kernel(**inputs):
    import numpy as np
    import concourse.bacc as bacc
    from concourse.bass_utils import run_bass_kernel_spmd

    a = {k: np.asarray(v) for k, v in inputs.items()}
    column = [a[k].reshape(NC, P).T for k in
              ("L0_conv_bq", "L0_conv_bk", "L1_conv_bias", "L1_conv_mask_weight", "L1_conv_filter")]
    arrays = {
        "x": a["x"].reshape(B, C, S),
        "wqT": a["L0_conv_Wq"].T,
        "wkT": a["L0_conv_Wk"].T,
        "wvT": a["L0_conv_Wv"].T,
        "chan": np.concatenate(column, axis=1),
        "bv": a["L0_conv_bv"],
        "wc": a["L1_conv_weight"].transpose(2, 3, 1, 0).reshape(9, C, C),
        "const": constants(np),
    }
    arrays = {k: np.ascontiguousarray(v) for k, v in arrays.items()}
    nc = bacc.Bacc("TRN2", target_bir_lowering=False, num_devices=1)
    args = [nc.dram_tensor(k, arrays[k].shape, mybir.dt.from_np(arrays[k].dtype), kind="ExternalInput").ap()
            for k in _INS]
    out = nc.dram_tensor("out", (B, C, S), F32, kind="ExternalOutput").ap()
    build(nc, *args, out)
    r = run_bass_kernel_spmd(nc, [arrays], core_ids=[0])
    return r.results[0]["out"].reshape(B, C, HW, HW)
```

```python
from contextlib import ExitStack

import concourse.bass as bass
from concourse import mybir

F32 = mybir.dt.float32
F16 = mybir.dt.float16
I32 = mybir.dt.int32
ALU = mybir.AluOpType
ACT = mybir.ActivationFunctionType
AX = mybir.AxisListType

P = 128
B, C, HW = 8, 512, 32
S = HW * HW
NC = C // P
HALF = 512
TOK = 128
D = 64
SEG = C // D
HPI = S // TOK
HPH = HALF // TOK
GRP = 16
WSCALE = 256.0
EPS = 1e-5
ROUND = 12582912.0
MAGIC = float(0x5F3759DF)
UNITS = SEG
MAX_QUOTA = [2, 2, 3, 3, 3, 2, 1, 0]

C_ID, C_GRP, C_ONE, C_IOTA, C_POS, C_END = 0, 128, 256, 320, 352, 384
B_Q, B_K, B_CONV, B_MASKW, B_FILT = 0, 4, 8, 12, 16


class Count:

    def __init__(self, per):
        self.n, self.per, self.i, self.entry = 0, per, None, 0

    def loop(self, i):
        self.i, self.entry = i, self.n

    def done(self, passes):
        assert self.n - self.entry == self.per, (self.n - self.entry, self.per)
        self.i, self.n = None, self.entry + self.per * passes

    def value(self):
        return self.n if self.i is None else self.i * self.per + self.n


def bank_turn(n, period, banks=3):
    left = (0, 4, 2)[period % banks]

    def bank_of(k):
        k %= period
        return k % banks if k < period - left else (k - period) % 2

    return bank_of(n), next(d for d in range(1, period) if bank_of(n - d) == bank_of(n))


def ring_items(u, nxt, prev, v_units, stat):
    first = sum(MAX_QUOTA[:u])
    tiles = [("max", first + k) for k in range(MAX_QUOTA[u])] if nxt else []
    at = {"a": tiles[0:1], "b": tiles[1:2], "c": tiles[2:]}
    at["d"] = [("value", u // 2)] if v_units and u % 2 else []
    if stat and u in (5, 6):
        at["d"].append(("stat", u - 5))
    if nxt and u == UNITS - 1:
        at["a"].append(("shift", 0))
    if prev and u == 1:
        at["d"].append(("den", 0))
    return at


def build(nc, x, wqT, wkT, wvT, chan, bv, wc, const, out):
    x_img = x.rearrange("b (c p) s -> b p c s", p=P)
    out_img = out.rearrange("b (c p) s -> b p c s", p=P)
    x1 = nc.dram_tensor("x1_scratch", (B, C, S), F32, kind="Internal").ap()
    wc_img = wc.rearrange("k (c p) n -> k p c n", p=P)
    recip_row = nc.dram_tensor("recip_scratch", (2, 512), F32, kind="Internal").ap()
    x1_img = x1.rearrange("b (c p) s -> b p c s", p=P)

    top = ExitStack()
    with top:
        def sem(name):
            return top.enter_context(nc.semaphore(name))

        def sb(stack, name, shape, dt):
            return stack.enter_context(nc.sbuf_tensor(name, shape, dt))

        cst = sb(top, "cst", [P, C_END], F32)
        prm = sb(top, "prm", [P, 20], F32)
        bn = sb(top, "bn", [P, NC, 2, 6], F32)
        mv = sb(top, "mv", [P, NC, 2], F32)
        gmv = sb(top, "gmv", [P, NC, 2], F32)
        dm = sb(top, "dm", [P, NC], F32)
        ve = sb(top, "ve", [P, NC], F32)
        nt = sb(top, "nt", [P, 2, NC], F32)
        rstd = sb(top, "rstd", [P, NC], F32)
        nbias = sb(top, "nbias", [P, NC], F32)
        xs = sb(top, "xs", [P, NC, S], F32)
        pad_mem = sb(top, "pad_mem", [P, 5120], F32)
        tab_mem = sb(top, "tab_mem", [P, 4, NC, HW], F32)
        mix_mem = sb(top, "mix_mem", [P, NC * (HW + 2) * (HW // 2)], F32)
        w_mem = sb(top, "w_mem", [P, 3, NC * C], F32)
        mxy = sb(top, "mxy", [P, 4, NC], F32)
        mwf = sb(top, "mwf", [P, NC], F32)
        ident = cst[:, C_ID:C_ID + P]
        grp = cst[:, C_GRP:C_GRP + P]
        ones = cst[:, C_ONE:C_ONE + D]

        bank = [top.enter_context(nc.psum_tensor(f"bank{k}", [P, 512], F32)) for k in range(8)]
        sc_bank = bank[0:3]
        v_ring = bank[3:6]
        pv_bank = bank[6]
        qk_bank = bank[7]

        s_const = sem("const_loaded")
        s_stat = sem("stat_step")
        s_passed = sem("passed")
        s1 = {n: sem(n) for n in (
            "w_loaded0", "w_loaded1", "w_hi_done", "w_split", "x_loaded", "x_first0", "x_first1", "x_first2",
            "x_first3", "xr_loaded0", "xr_loaded1", "kb_clear", "xn_ready", "xn_hi", "xn_split",
            "qk_ready", "qk_out", "qk_full", "qk_split", "qk_moved", "ring_full", "ring_free",
            "min_done", "shift_sent", "shift_row", "scores_full", "exp_done", "pv_done", "sum0", "sum1",
            "pv_out", "den_out", "den_in", "recip_done", "recip_out", "recip_in", "o_done", "resid_done", "x1_stored", "value_out")}

        def statistics(dve, xin, step):
            def chain(ins):
                ins.then_inc(s_stat, 1)
                step.n += 1

            def sync():
                dve.wait_ge(s_stat, step.value())

            def moments(c):
                for k in range(2):
                    chain(dve.bn_stats(bn[:, c, k], xin[:, c, k * 512:(k + 1) * 512]))

            def aggregate():
                sync()
                dve.sem_inc(s_passed, 1)
                for c in range(NC):
                    chain(dve.bn_aggr(mv[:, c], bn[:, c]))

            def centre(src, release):
                chain(dve.tensor_copy(gmv[:].rearrange("p c k -> p (c k)"), src[:, 0:2 * NC]))
                sync()
                dve.sem_inc(release, 1)
                chain(dve.tensor_tensor(dm[:], mv[:, :, 0], gmv[:, :, 0], ALU.subtract))
                sync()
                chain(dve.tensor_tensor(dm[:], dm[:], dm[:], ALU.mult))

            def finish(src, release):
                chain(dve.scalar_tensor_tensor(out=ve[:], in0=src[:, 0:NC], scalar=EPS, in1=gmv[:, :, 1],
                                               op0=ALU.add, op1=ALU.add))
                sync()
                dve.sem_inc(release, 1)
                chain(dve.tensor_scalar(nt[:, 0].bitcast(I32), ve[:].bitcast(I32), 1, None,
                                        ALU.logical_shift_right))
                sync()
                chain(dve.tensor_scalar(rstd[:].bitcast(I32), nt[:, 0].bitcast(I32), -1.0, MAGIC,
                                        ALU.mult, ALU.add))
                for _ in range(4):
                    sync()
                    chain(dve.tensor_tensor(nt[:, 0], rstd[:], rstd[:], ALU.mult))
                    sync()
                    chain(dve.scalar_tensor_tensor(out=nt[:, 1], in0=nt[:, 0], scalar=-0.5, in1=ve[:],
                                                   op0=ALU.mult, op1=ALU.mult))
                    sync()
                    chain(dve.scalar_tensor_tensor(out=rstd[:], in0=nt[:, 1], scalar=1.5, in1=rstd[:],
                                                   op0=ALU.add, op1=ALU.mult))
                sync()
                chain(dve.scalar_tensor_tensor(out=nbias[:], in0=gmv[:, :, 0], scalar=-1.0, in1=rstd[:],
                                               op0=ALU.mult, op1=ALU.mult))
            return moments, aggregate, centre, finish

        STAT_STEPS = 2 * NC + NC + 3 + 3 + 12 + 1
        STAT_AGG = 3 * NC
        STAT_DEV = STAT_AGG + 3

        def statistics_sum(pe, dst, k):
            if k == 0:
                return pe.matmul(dst[:, 0:2 * NC], grp, mv[:].rearrange("p c k -> p (c k)"),
                                 start=True, stop=True)
            return pe.matmul(dst[:, 0:NC], grp, dm[:], start=True, stop=True)

        st1 = ExitStack()
        w_hi, w_lo = (w_mem[:].rearrange("p a n -> p (a n)")[:, k * 3072:(k + 1) * 3072].bitcast(F16)
                      .rearrange("p (a c n) -> p a c n", a=3, c=NC) for k in range(2))
        bv_row = sb(st1, "bv_row", [P, C], F32)
        xn32 = tab_mem[:].rearrange("p a c n -> p (a c n)")
        xn_hi = mix_mem[:, 0:2048].bitcast(F16).rearrange("p (h c n) -> p h c n", h=2, c=NC)
        xn_lo = sb(st1, "xn_lo", [P, 2, NC, HALF], F16)
        val = [sb(st1, "val0", [P, HPH, C], F32)]
        xr = [sb(st1, "xr0", [P, NC, HALF], F32)]
        qk_hi, qk_lo = (pad_mem[:, k * 2048:(k + 1) * 2048].bitcast(F16)
                        .rearrange("p (a c n) -> p a c n", a=2, c=NC) for k in range(2))
        qk32 = pad_mem[:, 4096:5120].rearrange("p (a n) -> p a n", a=2)
        k_a = sb(st1, "k_a", [P, 2, SEG, HALF], F16)
        q_a = sb(st1, "q_a", [P, 2, SEG, HALF], F16)
        k_b = sb(st1, "k_b", [P, 2, SEG, HALF], F16)
        q_b = sb(st1, "q_b", [P, 2, SEG, HALF], F16)
        val.append(sb(st1, "val1", [P, HPH, C], F32))
        prob = sb(st1, "prob", [P, 8, 512], F32)
        psum_acc = sb(st1, "prob_sum", [P, 2, 2, 512], F32)
        nmax = sb(st1, "nmax", [P, SEG, 2], F32)
        nmin = sb(st1, "nmin", [P, SEG], F32)
        shift = sb(st1, "shift", [SEG, 2, TOK], F16)
        xr.append(sb(st1, "xr1", [P, NC, HALF], F32))
        pv_sb = sb(st1, "pv_sb", [P, 512], F32)
        den_sb = sb(st1, "den_sb", [P, 512], F32)
        den_col = sb(st1, "den_col", [P, 8], F32)
        recip_col = sb(st1, "recip_col", [P, 8], F32)
        q_av = q_a[:].rearrange("p h (j e) t -> p h e j t", e=2)
        q_bv = q_b[:].rearrange("p h (j e) t -> p h e j t", e=2)
        stage = prob[:].rearrange("p (a k) n -> p a k n", a=2)

        PER_RING = HPI * (16 + 1 + 1) + 2 * HPH + 2

        def tokens(s):
            return s // HPH, slice((s % HPH) * TOK, (s % HPH + 1) * TOK)

        st1.close()
        st2 = top.enter_context(ExitStack())
        PW = HW + 2
        PAIR = HW // 2
        filt = sb(st2, "filt", [P, 4, 2, 3, NC, C], F16)
        u_hi, u_lo = (filt[:, :, k] for k in range(2))
        v_hi = sb(st2, "v_hi", [P, 4, NC, PW, PAIR], F16)
        v_lo = sb(st2, "v_lo", [P, 4, NC, PW, PAIR], F16)
        xo = [xs[:], w_mem[:, 0:2].rearrange("p a (b n) -> p (a b) n", n=S)]
        xo_pair = [v.rearrange("p c (n two) -> p c n two", two=2) for v in xo]
        r_pad = pad_mem[:, 0:NC * PW * PW].rearrange("p (c h w) -> p c h w", c=NC, w=PW)
        rows, cols, wrow, wcol = (tab_mem[:, k] for k in range(4))
        v32_v = mix_mem[:].rearrange("p (c h w) -> p c h w", c=NC, w=PAIR)
        mask_v = mix_mem[:, 0:2 * S].rearrange("p (a h w) -> p a h w", a=2, w=HW)
        g0 = [w_mem[:, ky].rearrange("p (c n) -> p c n", n=C) for ky in range(3)]
        tail = NC * PW * PAIR * 4 - 2 * NC * C
        g12 = [v[:].rearrange("p a c h w -> p (a c h w)")[:, tail:].bitcast(F32)
               .rearrange("p (c n) -> p c n", n=C) for v in (v_hi, v_lo)]

        def filter_at(pos, ky):
            return (g0[ky], g12[ky % 2], g0[ky], g12[(ky + 1) % 2])[pos]

        s2 = {n: sem(n) for n in (
            "g0_loaded0", "g0_loaded1", "g0_loaded2", "g12_loaded0", "g12_loaded1", "g_summed", "g_less",
            "g_mixed", "u_cast", "u_split", "pad_clear", "x_in0", "x_in1",
            "sum2_full", "sum2_free", "mask_step", "tables", "r_normed", "bias_in", "mask_out", "mask_used",
            "relu_done", "v_made", "v_cast", "v_split", "conv_full", "conv_free", "y_stored0", "y_stored1")}
        MASK_STEPS = 2 * NC + 3 + 3 + 1 + 2 + 3 + 6 + 1
        V_OF = ((0, 2, ALU.subtract), (1, 3, ALU.subtract), (1, 2, ALU.add), (2, 1, ALU.subtract))
        Y_OF = (((0, 1),), ((1, -1),), ((0, 1), (1, 1)), ((0, 1), (1, -1)))
        FIRST_STATS = 8
        GROUPS = 4 * NC
        READS = tuple(len(y) for y in Y_OF)
        IMG_READS = NC * sum(READS)

        def reads_to(pos, co):
            if pos < 0:
                return co + 1
            return 4 + NC * sum(READS[:pos]) + READS[pos] * (co + 1)

        block = top.enter_context(nc.Block())

        @block.sync
        def _(sp):
            for c in range(NC):
                sp.dma_start(xs[:, c], x_img[0][:, c]).then_inc(s1[f"x_first{c}"], 16)
            sp.dma_start(cst[:], const).then_inc(s_const, 16)
            sp.dma_start(prm[:], chan).then_inc(s_const, 16)
            sp.dma_start(bv_row[:], bv.partition_broadcast(P)).then_inc(s_const, 16)
            for n, (k, w) in enumerate(((1, wkT), (0, wqT), (2, wvT))):
                if n == 2:
                    sp.wait_ge(s1["w_split"], 1)
                sp.dma_start(stage[:, n % 2], w.rearrange("(c p) n -> p c n", p=P)).then_inc(s1[f"w_loaded{n % 2}"], 16)
            sp.dma_start(xr[0][:], x_img[0][:, :, 0:HALF]).then_inc(s1["xr_loaded0"], 16)

            def move_qk(which, t, half, first=False):
                sp.wait_ge(s1["qk_split"], 2 + 8 * t + 4 * (which + 1))
                if not first:
                    sp.sem_inc(s_passed, 1)
                    sp.wait_ge(s1["exp_done"], 4 + 64 * (t - 1))
                hi_to = ((k_a, 0), (k_b, 0)) if which == 0 else ((q_a, 0), (q_a, D))
                lo_to = (k_a, D) if which == 0 else (q_b, 0)
                for e in range(2):
                    src = slice(e * D, (e + 1) * D)
                    for dst, p0 in hi_to:
                        sp.dma_start(dst[p0:p0 + D, half, e::2, :], qk_hi[src, which]).then_inc(s1["qk_moved"], 16)
                    dst, p0 = lo_to
                    sp.dma_start(dst[p0:p0 + D, half, e::2, :], qk_lo[src, which]).then_inc(s1["qk_moved"], 16)

            def send_shift(h, s):
                half, tok = tokens(s)
                sp.wait_ge(s1["shift_sent"], h + 1)
                sp.dma_start(q_b[D:D + 1, half, :, tok], shift[:, s % 2]).then_inc(s1["shift_row"], 16)

            def send_sums(h):
                sp.wait_ge(s1["den_out"], h + 1)
                for e in range(2):
                    sp.dma_start(den_col[e * D:(e + 1) * D], den_sb[e * D:e * D + 1].rearrange("a (p n) -> a p n", n=8))\
                        .then_inc(s1["den_in"], 16)
                sp.wait_ge(s1["recip_done"], h + 1)
                sp.dma_start(recip_row.rearrange("e (p n) -> (e p) n", n=8), recip_col[:]).then_inc(s1["recip_out"], 16)
                sp.wait_ge(s1["recip_out"], 16 * (h + 1))
                for e in range(2):
                    sp.dma_start(den_sb[e * D:(e + 1) * D], recip_row[e].partition_broadcast(D))\
                        .then_inc(s1["recip_in"], 16)

            def store_x1(t, img, half):
                sp.wait_ge(s1["resid_done"], 1 + 4 * (t + 1))
                sp.sem_inc(s_passed, 1)
                sp.dma_start(x1_img[img][:, :, half * HALF:(half + 1) * HALF], xr[half][:]).then_inc(s1["x1_stored"], 16)

            def slot(img, s, prev=True, nxt=True, more=True):
                t = img * 2 + s // HPH
                r = s % HPH
                if s == 1:
                    sp.wait_ge(s1["xn_hi"], 8 * (img + 1))
                    sp.dma_start(xs[:], x_img[img + 1] if more else x1_img[0]).then_inc(s1["x_loaded"], 16)
                if s == 5 and not more:
                    sp.wait_ge(s1["value_out"], B * HPI)
                    for ky in range(3):
                        sp.dma_start(g0[ky], wc_img[3 * ky]).then_inc(s2[f"g0_loaded{ky}"], 16)
                if r == 1 and (s < HPH or more):
                    move_qk(0, t + 1, 1 - s // HPH)
                if r == 2 and (s < HPH or more):
                    move_qk(1, t + 1, 1 - s // HPH)
                if r == 1 and (s < HPH or more):
                    sp.wait_ge(s1["x1_stored"], 16 + 16 * t)
                    if s < HPH:
                        src = x_img[img][:, :, HALF:S]
                    else:
                        src = x_img[img + 1][:, :, 0:HALF]
                    sp.dma_start(xr[1 - s // HPH][:], src).then_inc(s1[f"xr_loaded{1 - s // HPH}"], 16)
                if prev:
                    send_sums(img * HPI + s - 1)
                if nxt:
                    send_shift(img * HPI + s + 1, (s + 1) % HPI)
                if r == 0 and prev:
                    if s == 0:
                        store_x1(t - 1, img - 1, 1)
                    else:
                        store_x1(t - 1, img, 0)

            sp.sem_inc(s1["x1_stored"], 16)
            sp.wait_ge(s1["kb_clear"], 6)
            move_qk(0, 0, 0, first=True)
            move_qk(1, 0, 0, first=True)
            send_shift(0, 0)
            slot(0, 0, prev=False)
            with sp.Fori(0, B - 1) as i:
                for s in range(1, HPI):
                    slot(i, s)
                slot(i + 1, 0)
            for s in range(1, HPI):
                slot(B - 1, s, nxt=s < HPI - 1, more=False)
            send_sums(B * HPI - 1)
            def load_column(kx, ky):
                sp.dma_start(g12[ky % 2], wc_img[3 * ky + kx]).then_inc(s2[f"g12_loaded{ky % 2}"], 16)

            load_column(2, 0)
            store_x1(2 * B - 1, B - 1, 1)
            sp.wait_ge(s1["x1_stored"], 16 + 16 * 2 * B)
            load_column(2, 1)
            sp.wait_ge(s2["u_split"], 4)
            sp.wait_ge(s2["g_summed"], 1)
            load_column(2, 2)
            sp.wait_ge(s2["u_split"], 6)
            load_column(1, 0)
            for ky in range(1, 3):
                sp.wait_ge(s2["u_split"], 6 + 2 * ky - 1)
                load_column(1, ky)
                if ky == 2:
                    sp.wait_ge(s2["u_split"], 10)
                    sp.dma_start(xo[1], x1_img[1]).then_inc(s2["x_in1"], 16)

            def store_image(img, b, load):
                for co in range(NC):
                    sp.wait_ge(s2["conv_free"], IMG_READS * img + reads_to(3, co))
                    sp.dma_start(out_img[img][:, co], xo[b][:, co]).then_inc(s2[f"y_stored{b}"], 16)
                if load is not None:
                    sp.wait_ge(s2[f"y_stored{b}"], 16 * NC * load)
                    sp.dma_start(xo[b], x1_img[img + 2]).then_inc(s2[f"x_in{b}"], 16)

            with sp.Fori(0, B // 2 - 1) as j:
                for b in range(2):
                    store_image(j * 2 + b, b, j + 1)
            for b in range(2):
                store_image(B - 2 + b, b, None)
            for b in range(2):
                sp.wait_ge(s2[f"y_stored{b}"], 16 * NC * (B // 2))

        @block.tensor
        def _(pe):
            ring = Count(PER_RING)

            def take():
                b, ago = bank_turn(ring.n, PER_RING)
                if ring.n >= ago:
                    pe.wait_ge(s1["ring_free"], ring.value() + 3 - ago)
                dst = v_ring[b]
                ring.n += 1
                return dst

            def stat_item(img, k):
                dst = take()
                pe.wait_ge(s_stat, img * STAT_STEPS + (STAT_AGG, STAT_DEV)[k])
                statistics_sum(pe, dst, k).then_inc(s1["ring_full"], 1)

            def project_qk(t, half, which, j, first=False):
                w = 1 - which
                pe.wait_ge(s1["xn_split"], 2 + 4 * (t + 1))
                dst = qk_bank
                if first:
                    dst = (qk_bank, pv_bank)[j % 2]
                    if which + j > 0:
                        pe.wait_ge(s1["qk_out"], 4 * which + j)
                else:
                    pe.wait_ge(s1["qk_out"], 8 * t + 4 * which + j + 1)
                steps = [(a, b, c) for c in range(NC) for a, b in
                         ((w_hi, xn_hi), (w_hi, xn_lo), (w_lo, xn_hi))]
                for n, (a, b, c) in enumerate(steps):
                    mm = pe.matmul(dst[:], a[:, w, c, j * P:(j + 1) * P], b[:, half, c],
                                   start=(n == 0), stop=(n == len(steps) - 1))
                mm.then_inc(s1["qk_ready"], 1)

            def project_value(t, half, g):
                pe.wait_ge(s1["xn_split"], 2 + 4 * (t + 1))
                dst = take()
                steps = [(a, b, c) for c in range(NC) for a, b in
                         ((xn_hi, w_hi), (xn_hi, w_lo), (xn_lo, w_hi))]
                for n, (a, b, c) in enumerate(steps):
                    mm = pe.matmul(dst[:], a[:, half, c, g * TOK:(g + 1) * TOK], b[:, 2, c],
                                   start=(n == 0), stop=(n == len(steps) - 1))
                mm.then_inc(s1["ring_full"], 1)

            def max_tile(s, m):
                half, tok = tokens(s)
                dst = take()
                pe.matmul(dst[:].rearrange("p (k t) -> p k t", t=TOK), q_a[:, half, m // 2, tok],
                          k_a[:, half, 4 * (m % 2):4 * (m % 2) + 4, tok],
                          start=True, stop=True).then_inc(s1["ring_full"], 1)

            def shift_item(h):
                dst = take()
                pe.wait_ge(s1["min_done"], h + 1)
                pe.matmul(dst[0:SEG, 0:TOK], nmin[:], ident, start=True, stop=True).then_inc(s1["ring_full"], 1)

            def den_item(h, par):
                dst = take()
                pe.wait_ge(s1["sum0"], 7 + 7 * (h + 1))
                pe.matmul(dst[0:D, :], ones, psum_acc[:, par, 0], start=True, stop=True)
                pe.wait_ge(s1["sum1"], 7 + 7 * (h + 1))
                pe.matmul(dst[D:P, :], ones, psum_acc[:, par, 1], start=True, stop=True).then_inc(s1["ring_full"], 1)

            def scores(h, s, u, part):
                half, tok = tokens(s)
                k_op, q_op = ((k_a, q_av), (k_b, q_bv))[part]
                for e in range(2):
                    b, ago = bank_turn(s * 16 + u * 2 + e, 16 * HPI)
                    if part == 0:
                        pe.wait_ge(s1["exp_done"], 16 * h + 2 * u + e + 5 - ago)
                    mm = pe.matmul(sc_bank[b][:].rearrange("p (j t) -> p j t", t=TOK), k_op[:, half, u, tok],
                                   q_op[:, half, e, :, tok], start=(part == 0), stop=(part == 1))
                    if part == 1:
                        mm.then_inc(s1["scores_full"], 1)

            def weigh(h, s, kc):
                if kc == 0:
                    pe.wait_ge(s1["pv_out"], h + 1)
                    pe.wait_ge(s1["value_out"], h + 1)
                for e in range(2):
                    pe.wait_ge(s1["exp_done"], 4 + 16 * h + 2 * kc + e + 1)
                    pe.matmul(pv_bank[e * D:(e + 1) * D, :], val[s // HPH][:, s % HPH, kc * D:(kc + 1) * D],
                              prob[:, (2 * kc + e) % 8], start=(kc == 0),
                              stop=(kc == SEG - 1)).then_inc(s1["pv_done"], 1)

            def slot(img, s, prev=True, nxt=True, more=True):
                h = img * HPI + s
                t = img * 2 + s // HPH
                r = s % HPH
                proj = r < 3 and (s < HPH or more)
                for u in range(UNITS):
                    items = ring_items(u, nxt, prev, proj and r == 2, s == 2)

                    def run(place):
                        for kind, a in items[place]:
                            if kind == "max":
                                max_tile((s + 1) % HPI, a)
                            elif kind == "value":
                                project_value(t + 1, 1 - s // HPH, a)
                            elif kind == "stat":
                                stat_item(img + 1, a)
                            elif kind == "shift":
                                shift_item(h + 1)
                            else:
                                den_item(h - 1, (s - 1) % 2)
                    if u == 0 and nxt and r == 3:
                        pe.wait_ge(s1["qk_moved"], 192 * (t + 2))
                    run("a")
                    scores(h, s, u, 0)
                    run("b")
                    if u == 0:
                        pe.wait_ge(s1["shift_row"], 16 * (h + 1))
                    scores(h, s, u, 1)
                    run("c")
                    if proj and r < 2 and u % 2:
                        project_qk(t + 1, 1 - s // HPH, r, u // 2)
                    run("d")
                    if u == 0 and prev:
                        weigh(h - 1, (s - 1) % HPI, SEG - 1)
                    if u == 2:
                        weigh(h, s, 0)
                    if u >= 2:
                        weigh(h, s, u - 1)

            pe.sem_inc(s1["pv_done"], 8)
            pe.sem_inc(s2["conv_full"], GROUPS)
            pe.wait_ge(s_const, 48)
            stat_item(0, 0)
            stat_item(0, 1)
            for which in range(2):
                pe.wait_ge(s1["w_split"], which + 1)
                for j in range(NC):
                    project_qk(0, 0, which, j, first=True)
            pe.wait_ge(s1["w_split"], 3)
            for g in range(HPH):
                project_value(0, 0, g)
            pe.wait_ge(s1["qk_moved"], 192)
            for m in range(16):
                max_tile(0, m)
            shift_item(0)
            slot(0, 0, prev=False)
            with pe.Fori(0, B - 1) as i:
                ring.loop(i)
                for s in range(1, HPI):
                    slot(i, s)
                slot(i + 1, 0)
            ring.done(B - 1)
            for s in range(1, HPI):
                slot(B - 1, s, nxt=s < HPI - 1, more=False)
            weigh(B * HPI - 1, HPI - 1, SEG - 1)
            den_item(B * HPI - 1, 1)

            pe.wait_ge(s1["pv_out"], B * HPI + 1)
            pe.wait_ge(s1["den_out"], B * HPI)

            def stat2(img, k):
                pe.wait_ge(s2["sum2_free"], (img - 1) * 2 + k + 1)
                pe.wait_ge(s_stat, STAT_STEPS * B + img * STAT_STEPS + (STAT_AGG, STAT_DEV)[k])
                statistics_sum(pe, qk_bank, k).then_inc(s2["sum2_full"], 1)

            def convolve(img, more=True, stats=3):
                for pos in range(4):
                    pe.wait_ge(s2["u_split"], (3, 6, 12, 12)[pos])
                    pe.wait_ge(s2["v_split"], img * 4 + pos + 2)
                    for co in range(NC):
                        pe.wait_ge(s2["conv_free"], IMG_READS * img + reads_to(pos - 1, co))
                        steps = [(ky, c, u, v) for ky in range(3) for c in range(NC) for u, v in
                                 ((u_hi, v_hi), (u_hi, v_lo), (u_lo, v_hi))]
                        for n, (ky, c, u, v) in enumerate(steps):
                            mm = pe.matmul(bank[co][:].rearrange("p (h w) -> p h w", w=PAIR),
                                           u[:, pos, ky, c, co * P:(co + 1) * P],
                                           v[:, pos, c, ky:ky + HW, :],
                                           start=(n == 0), stop=(n == len(steps) - 1))
                        mm.then_inc(s2["conv_full"], 1)
                        if more and pos * NC + co in (stats, stats + 1):
                            stat2(img + 1, pos * NC + co - stats)

            convolve(0, stats=FIRST_STATS)
            with pe.Fori(1, B - 1) as i:
                convolve(i)
            convolve(B - 1, more=False)

        @block.scalar
        def _(act):
            def normed(img, half, c, first=False):
                k = 4 * half + c
                act.wait_ge(s_stat, (img + 1) * STAT_STEPS)
                dst = xn32
                if first:
                    dst = psum_acc[:, c // 2, c % 2]
                    if half == 1:
                        act.wait_ge(s1["xn_split"], k - 1)
                else:
                    act.wait_ge(s1["xn_split"], img * 8 + k + 2)
                act.activation(dst, xs[:, c, half * HALF:(half + 1) * HALF], ACT.Identity,
                               bias=nbias[:, c:c + 1], scale=rstd[:, c:c + 1]).then_inc(s1["xn_ready"], 1)
                act.activation(xn_hi[:, half, c], xs[:, c, half * HALF:(half + 1) * HALF], ACT.Identity,
                               bias=nbias[:, c:c + 1], scale=rstd[:, c:c + 1]).then_inc(s1["xn_hi"], 1)

            def qk_evacuate(t, which, j, first=False):
                act.wait_ge(s1["qk_ready"], 8 * t + 4 * which + j + 1)
                act.wait_ge(s1["qk_split"], 8 * t + 4 * which + j + 1)
                col = (B_K, B_Q)[which] + j
                src = pv_bank if first and j % 2 else qk_bank
                act.activation(qk32[:, j % 2], src[:], ACT.Identity, bias=prm[:, col:col + 1],
                               scale=1.0 / WSCALE).then_inc(s1["qk_full"], 1)
                if j == 0 and not first:
                    act.wait_ge(s1["qk_moved"], 192 * t)
                act.activation(qk_hi[:, which, j], src[:], ACT.Identity, bias=prm[:, col:col + 1],
                               scale=1.0 / WSCALE).then_inc(s1["qk_out"], 1)

            def exp_tile(h, s, u, e):
                act.wait_ge(s1["scores_full"], 16 * h + 2 * u + e + 1)
                act.wait_ge(s1["pv_done"], 16 * h + 2 * u + e + 1)
                act.wait_ge(s1[f"sum{e}"], 7 * h + (u + 4 if u < 4 else 7 + max(u - 4, 1)))
                act.activation(prob[:, (2 * u + e) % 8], sc_bank[bank_turn(s * 16 + 2 * u + e, 16 * HPI)[0]][:], ACT.Exp,
                               scale=float(D) ** -0.5).then_inc(s1["exp_done"], 1)

            def evacuate_pv(h):
                act.wait_ge(s1["pv_done"], 8 + 16 * (h + 1))
                act.wait_ge(s1["o_done"], h + 1)
                act.activation(pv_sb[:], pv_bank[:], ACT.Copy).then_inc(s1["pv_out"], 1)

            def cast_filters(pos, ky):
                if pos == 0:
                    act.wait_ge(s2[f"g0_loaded{ky}"], 16)
                elif pos == 1:
                    act.wait_ge(s2[f"g12_loaded{ky % 2}"], 16 * (ky // 2 + 1))
                else:
                    act.wait_ge(s2["g_mixed" if pos == 2 else "g_less"], ky + 1)
                act.activation(u_hi[:, pos, ky], filter_at(pos, ky), ACT.Copy,
                               scale=WSCALE if pos < 2 else WSCALE / 2).then_inc(s2["u_cast"], 1)

            def norm_chunk(img, b, c):
                act.activation(r_pad[:, c, 1:HW + 1, 1:HW + 1], xo[b][:, c].rearrange("p (h w) -> p h w", w=HW),
                               ACT.Identity, bias=nbias[:, c:c + 1], scale=rstd[:, c:c + 1])\
                    .then_inc(s2["r_normed"], 1)

            def bias_chunk(img, b, c):
                act.wait_ge(s2["r_normed"], 4 * img + 4)
                act.activation(xo[b][:, c], xo[b][:, c], ACT.Identity, bias=prm[:, B_CONV + c:B_CONV + c + 1],
                               scale=1.0).then_inc(s2["bias_in"], 1)

            def relu(img, c):
                act.wait_ge(s2["mask_used"], 4 * img + c + 1)
                act.activation(r_pad[:, c, 1:HW + 1, 1:HW + 1], r_pad[:, c, 1:HW + 1, 1:HW + 1], ACT.Relu)\
                    .then_inc(s2["relu_done"], 1)

            def cast_v(img, pos):
                act.wait_ge(s2["v_made"], 4 * img + pos + 2)
                act.wait_ge(s2["conv_full"], GROUPS * img + NC * (pos + 1))
                act.activation(v_hi[:, pos], v32_v, ACT.Copy).then_inc(s2["v_cast"], 1)

            def slot(img, s, prev=True, more=True):
                h = img * HPI + s
                t = img * 2 + s // HPH
                r = s % HPH
                for u in range(UNITS):
                    exp_tile(h, s, u, 0)
                    exp_tile(h, s, u, 1)
                    if u == 0 and prev:
                        evacuate_pv(h - 1)
                    if r < 2 and u % 2 and (s < HPH or more):
                        qk_evacuate(t + 1, r, u // 2)
                    if s == 3 and more and u >= 4:
                        normed(img + 1, 0, u - 4)
                    if s == 7 and more and u < 4:
                        normed(img + 1, 1, u)
                    if s == 4 and not more and u < 4:
                        if u == 0:
                            act.wait_ge(s_stat, STAT_STEPS * (B + 1))
                            act.wait_ge(s2["pad_clear"], 1)
                        norm_chunk(0, 0, u)
                    if s == 4 and not more and u >= 4:
                        bias_chunk(0, 0, u - 4)
                    if s == 7 and not more and u < 3:
                        if u == 0:
                            act.wait_ge(s1["value_out"], B * HPI)
                            act.wait_ge(s1["x1_stored"], 16 * 2 * B)
                        cast_filters(0, u)
                    if s == 7 and not more and 3 <= u < 7:
                        relu(0, u - 3)

            act.sem_inc(s1["exp_done"], 4)
            act.sem_inc(s1["qk_out"], 1)
            act.sem_inc(s1["pv_out"], 1)
            act.wait_ge(s_const, 48)
            for c in range(NC):
                normed(0, 0, c, first=True)
            for which in range(2):
                for j in range(NC):
                    qk_evacuate(0, which, j, first=True)
            for c in range(NC):
                normed(0, 1, c, first=True)
            slot(0, 0, prev=False)
            with act.Fori(0, B - 1) as i:
                for s in range(1, HPI):
                    slot(i, s)
                slot(i + 1, 0)
            for s in range(1, HPI):
                slot(B - 1, s, more=False)
            evacuate_pv(B * HPI - 1)

            def prepare(img, b):
                act.wait_ge(s_stat, STAT_STEPS * B + (img + 1) * STAT_STEPS)
                act.wait_ge(s2["v_made"], 4 * img + 1)
                for c in range(NC):
                    norm_chunk(img, b, c)
                for c in range(NC):
                    bias_chunk(img, b, c)
                for c in range(NC):
                    relu(img, c)
                for pos in range(3):
                    cast_v(img, pos)

            act.wait_ge(s1["sum1"], 7 + 7 * B * HPI)
            act.wait_ge(s1["den_out"], B * HPI)
            cast_v(0, 0)
            for ky in range(3):
                cast_filters(1, ky)
            cast_v(0, 1)
            for ky in range(3):
                cast_filters(3, ky)
                cast_filters(2, ky)
            act.wait_ge(s2["u_split"], 12)
            act.sem_inc(s_passed, 1)
            cast_v(0, 2)
            cast_v(0, 3)
            prepare(1, 1)
            with act.Fori(0, B // 2 - 1) as j:
                for b in range(2):
                    cast_v(j * 2 + b + 1, 3)
                    prepare(j * 2 + b + 2, b)
            cast_v(B - 1, 3)

        @block.gpsimd
        def _(pool):
            def add_tile(h, s, kc):
                pool.wait_ge(s1["exp_done"], 4 + 16 * h + 2 * kc + 2)
                acc = psum_acc[:, s % 2, 1]
                pool.wait_ge(s1["sum1"], 7 + 7 * h + kc - 1)
                in0 = prob[:, 1] if kc == 1 else acc
                nc.gpsimd.tensor_tensor(acc, in0, prob[:, (2 * kc + 1) % 8], ALU.add).then_inc(s1["sum1"], 1)

            def divide(h):
                pool.wait_ge(s1["pv_out"], 1 + h + 1)
                pool.wait_ge(s1["recip_in"], 32 * (h + 1))
                nc.gpsimd.tensor_tensor(den_sb[:], pv_sb[:], den_sb[:], ALU.mult).then_inc(s1["o_done"], 1)

            def residual(h, s):
                half, tok = tokens(s)
                pool.wait_ge(s1["o_done"], 1 + h + 1)
                o_v = den_sb[:].rearrange("p (j t) -> p j t", t=TOK)
                nc.gpsimd.tensor_tensor(xr[half][:, :, tok], xr[half][:, :, tok], o_v, ALU.add)\
                    .then_inc(s1["resid_done"], 1)

            def mask_chunk(img, c):
                if c == 0:
                    pool.wait_ge(s2["tables"], img + 1)
                    pool.wait_ge(s2["v_split"], 4 * img + 1)
                if c >= 2:
                    pool.wait_ge(s2["mask_used"], 4 * img + c - 1)
                nc.gpsimd.tensor_tensor(mask_v[:, c % 2], wrow[:, c].unsqueeze(2).broadcast_to([P, HW, HW]),
                                        wcol[:, c].unsqueeze(1).broadcast_to([P, HW, HW]), ALU.subtract)\
                    .then_inc(s2["mask_out"], 1)

            def slot(img, s, prev=True, more=True):
                h = img * HPI + s
                for u in range(UNITS):
                    if s == 3 and u == 4 and not more:
                        pool.wait_ge(s1["qk_moved"], 192 * 2 * B)
                        nc.gpsimd.memset(pad_mem[:], 0.0).then_inc(s2["pad_clear"], 1)
                    if s == 7 and 1 <= u < 5 and not more:
                        mask_chunk(0, u - 1)
                    if u == 0 and prev:
                        add_tile(h - 1, (s - 1) % HPI, SEG - 1)
                    if u >= 2:
                        add_tile(h, s, u - 1)
                    if u == 6 and prev:
                        divide(h - 1)
                    if u == 7 and prev:
                        if s % HPH == 1:
                            pool.wait_ge(s1[f"xr_loaded{s // HPH}"], 16 * (img + 1))
                        residual(h - 1, (s - 1) % HPI)

            nc.gpsimd.memset(k_b[D:P], 0.0).then_inc(s1["kb_clear"], 1)
            nc.gpsimd.memset(q_b[D:P], 0.0).then_inc(s1["kb_clear"], 1)
            pool.wait_ge(s1["kb_clear"], 2)
            nc.gpsimd.memset(k_b[D:D + 1], 8.0).then_inc(s1["kb_clear"], 4)
            pool.sem_inc(s1["sum1"], 7)
            pool.sem_inc(s1["resid_done"], 1)
            slot(0, 0, prev=False)
            with pool.Fori(0, B - 1) as i:
                for s in range(1, HPI):
                    slot(i, s)
                slot(i + 1, 0)
            for s in range(1, HPI):
                slot(B - 1, s, more=False)
            add_tile(B * HPI - 1, HPI - 1, SEG - 1)
            divide(B * HPI - 1)
            residual(B * HPI - 1, HPI - 1)

            for ky in range(3):
                pool.wait_ge(s2["g_less"], ky + 1)
                nc.gpsimd.tensor_tensor(g0[ky], g0[ky], g12[ky % 2], ALU.add).then_inc(s2["g_mixed"], 1)
            with pool.Fori(1, B) as i:
                for c in range(NC):
                    mask_chunk(i, c)

        @block.vector
        def _(dve):
            ring = Count(PER_RING)
            step = Count(STAT_STEPS)

            def item():
                dve.wait_ge(s1["ring_full"], ring.value() + 1)
                src = v_ring[bank_turn(ring.n, PER_RING)[0]]
                ring.n += 1
                return src

            moments, aggregate, centre, finish = statistics(dve, xs, step)

            def split_norm(img, half, c, first=False):
                src = psum_acc[:, c // 2, c % 2] if first else xn32
                k = 4 * half + c
                dve.wait_ge(s1["xn_ready"], img * 8 + k + 1)
                dve.wait_ge(s1["xn_hi"], img * 8 + k + 1)
                dve.tensor_tensor(xn_lo[:, half, c], src, xn_hi[:, half, c], ALU.subtract)\
                    .then_inc(s1["xn_split"], 1)

            def split_qk(t, which, j):
                n = 8 * t + 4 * which + j
                dve.wait_ge(s1["qk_full"], n + 1)
                dve.wait_ge(s1["qk_out"], 1 + n + 1)
                dve.tensor_tensor(qk_lo[:, which, j], qk32[:, j % 2], qk_hi[:, which, j], ALU.subtract)\
                    .then_inc(s1["qk_split"], 1)

            def add_tile(h, s, kc):
                dve.wait_ge(s1["exp_done"], 4 + 16 * h + 2 * kc + 1)
                acc = psum_acc[:, s % 2, 0]
                dve.wait_ge(s1["sum0"], 7 + 7 * h + kc - 1)
                in0 = prob[:, 0] if kc == 1 else acc
                dve.tensor_tensor(acc, in0, prob[:, (2 * kc) % 8], ALU.add).then_inc(s1["sum0"], 1)

            def max_item(h, m):
                src = item()
                if m == 0:
                    dve.wait_ge(s1["min_done"], h)
                dve.tensor_reduce(nmax[:, m // 2, m % 2:m % 2 + 1], src[:], AX.X, ALU.max, negate=True)\
                    .then_inc(s1["ring_free"], 1)
                if m == 15:
                    dve.wait_ge(s1["ring_free"], 2 + ring.value())
                    dve.tensor_tensor(nmin[:], nmax[:, :, 0], nmax[:, :, 1], ALU.min).then_inc(s1["min_done"], 1)

            def shift_item(h, s):
                src = item()
                if s > 0:
                    dve.wait_ge(s1["shift_row"], 16 * (h - 1))
                dve.tensor_scalar(shift[:, s % 2], src[0:SEG, 0:TOK], 0.125, None, ALU.mult)\
                    .then_inc(s1["shift_sent"], 1)
                dve.wait_ge(s1["shift_sent"], h + 1)
                dve.sem_inc(s1["ring_free"], 1)

            def value_item(h, half, g):
                src = item()
                dve.scalar_tensor_tensor(out=val[half][:, g], in0=src[:], scalar=1.0 / WSCALE, in1=bv_row[:],
                                         op0=ALU.mult, op1=ALU.add).then_inc(s1["value_out"], 1)
                dve.wait_ge(s1["value_out"], h + 1)
                dve.sem_inc(s1["ring_free"], 1)

            def den_item(h):
                src = item()
                dve.wait_ge(s1["resid_done"], h + 1)
                dve.tensor_copy(den_sb[:], src[:]).then_inc(s1["den_out"], 1)
                dve.wait_ge(s1["den_out"], h + 1)
                dve.sem_inc(s1["ring_free"], 1)

            def invert_sums(h):
                dve.wait_ge(s1["den_in"], 32 * (h + 1))
                dve.wait_ge(s1["resid_done"], h + 1)
                dve.reciprocal(recip_col[:], den_col[:]).then_inc(s1["recip_done"], 1)

            def stat_item(img, k):
                src = item()
                (centre, finish)[k](src, s1["ring_free"])

            def split_filters(pos, ky, k):
                dve.wait_ge(s2["u_cast"], k + 1)
                dve.scalar_tensor_tensor(out=u_lo[:, pos, ky], in0=filter_at(pos, ky),
                                         scalar=WSCALE if pos < 2 else WSCALE / 2,
                                         in1=u_hi[:, pos, ky], op0=ALU.mult, op1=ALU.subtract)\
                    .then_inc(s2["u_split"], 1)

            mstep = Count(MASK_STEPS)
            mstep.n = 0

            def chain(ins):
                ins.then_inc(s2["mask_step"], 1)
                mstep.n += 1

            def sync():
                dve.wait_ge(s2["mask_step"], mstep.value())

            iota = cst[:, C_IOTA:C_IOTA + HW].unsqueeze(1).broadcast_to([P, NC, HW])
            place = cst[:, C_POS:C_POS + HW].unsqueeze(1).broadcast_to([P, NC, HW])

            def over_hw(v):
                return v.unsqueeze(2).broadcast_to([P, NC, HW])

            def sums(img, c):
                if c == 0:
                    dve.wait_ge(s2["r_normed"], 4 * img + 4)
                    dve.sem_inc(s_passed, 1)
                v = r_pad[:, c, 1:HW + 1, 1:HW + 1]
                chain(dve.tensor_reduce(rows[:, c], v, AX.X, ALU.add))
                chain(dve.tensor_reduce(cols[:, c], v.rearrange("p h w -> p w h"), AX.X, ALU.add))

            def make_tables():
                sync()
                chain(dve.tensor_tensor(wrow, rows, iota, ALU.mult))
                chain(dve.tensor_tensor(wcol, cols, iota, ALU.mult))
                chain(dve.tensor_reduce(mxy[:, 2], rows, AX.X, ALU.add))
                sync()
                chain(dve.tensor_reduce(mxy[:, 0], wrow, AX.X, ALU.add))
                chain(dve.tensor_reduce(mxy[:, 1], wcol, AX.X, ALU.add))
                chain(dve.tensor_scalar(mxy[:, 2], mxy[:, 2], 1e-9, None, ALU.max))
                sync()
                chain(dve.reciprocal(mxy[:, 3], mxy[:, 2]))
                sync()
                for a in range(2):
                    chain(dve.tensor_tensor(mxy[:, a], mxy[:, a], mxy[:, 3], ALU.mult))
                sync()
                chain(dve.tensor_scalar(mxy[:, 0:2], mxy[:, 0:2], 1.0, float(HW), ALU.max, ALU.min))
                sync()
                chain(dve.tensor_scalar(mxy[:, 0:2], mxy[:, 0:2], ROUND, ROUND, ALU.add, ALU.subtract))
                sync()
                chain(dve.tensor_scalar(mxy[:, 0:2], mxy[:, 0:2], 2.0 / (HW - 1), -1.0 - 2.0 / (HW - 1),
                                        ALU.mult, ALU.add))
                sync()
                for a, w in enumerate((wrow, wcol)):
                    chain(dve.tensor_tensor(w, place, over_hw(mxy[:, a]), ALU.subtract))
                sync()
                for w in (wrow, wcol):
                    chain(dve.scalar_tensor_tensor(out=w, in0=w, scalar=-1.0, in1=w,
                                                   op0=ALU.mult, op1=ALU.max))
                sync()
                for w in (wrow, wcol):
                    chain(dve.tensor_tensor(w, w, over_hw(mwf[:]), ALU.mult))
                sync()
                chain(dve.tensor_scalar(wrow, wrow, -1.0, 1.0, ALU.mult, ALU.add))
                sync()
                dve.sem_inc(s2["tables"], 1)

            def mask_chunk(img, c):
                dve.wait_ge(s2["mask_out"], 4 * img + c + 1)
                v = r_pad[:, c, 1:HW + 1, 1:HW + 1]
                dve.scalar_tensor_tensor(out=v, in0=mask_v[:, c % 2], scalar=-1.0, in1=v,
                                         op0=ALU.max, op1=ALU.mult).then_inc(s2["mask_used"], 1)

            def make_v(img, pos):
                if pos == 0:
                    dve.wait_ge(s2["relu_done"], 4 * img + 4)
                dve.wait_ge(s2["v_split"], 4 * img + pos + 1)
                a, b, op = V_OF[pos]
                d = [r_pad[:, :, :, k:k + HW - 1:2] for k in range(4)]
                dve.tensor_tensor(v32_v, d[a], d[b], op).then_inc(s2["v_made"], 1)

            def slot(img, s, prev=True, nxt=True, more=True):
                h = img * HPI + s
                t = img * 2 + s // HPH
                r = s % HPH
                proj = r < 3 and (s < HPH or more)
                for u in range(UNITS):
                    if not more:
                        if s == 4 and u == 7:
                            chain(dve.tensor_scalar(mwf[:], prm[:, B_FILT:B_FILT + NC], 1.0, None, ALU.is_equal))
                            sync()
                            chain(dve.tensor_tensor(mwf[:], mwf[:], prm[:, B_MASKW:B_MASKW + NC], ALU.mult))
                        if s in (5, 6) and u >= 6:
                            sums(0, 2 * (s - 5) + u - 6)
                        if s == 7 and u == 0:
                            make_tables()
                        if s == 7 and 2 <= u < 6:
                            mask_chunk(0, u - 2)
                        if s == 7 and u in (1, 6):
                            split_filters(0, u // 6, u // 6)
                        if s == 7 and u == 7:
                            make_v(0, 0)
                    if s == 2 and u == 5:
                        aggregate()
                    items = ring_items(u, nxt, prev, proj and r == 2, s == 2)
                    for place in "abcd":
                        if place == "c":
                            if s == 3 and more and u >= 5:
                                split_norm(img + 1, 0, u - 5)
                            if s == 4 and more and u == 0:
                                split_norm(img + 1, 0, 3)
                            if s == 7 and more and 1 <= u < 5:
                                split_norm(img + 1, 1, u - 1)
                        if place == "d" and u == 0 and prev:
                            add_tile(h - 1, (s - 1) % HPI, SEG - 1)
                        if place == "d" and u >= 2:
                            add_tile(h, s, u - 1)
                        if place == "d" and s == 1 and u in (3, 5, 7):
                            if u == 3:
                                dve.wait_ge(s1["x_loaded"], 16 * (img + 1))
                            for c in (u // 2 - 1,) if u < 7 else (2, 3):
                                moments(c)
                        for kind, a in items[place]:
                            if kind == "max":
                                max_item(h + 1, a)
                            elif kind == "value":
                                value_item(4 * (t + 1) + a, 1 - s // HPH, a)
                            elif kind == "stat":
                                stat_item(img + 1, a)
                            elif kind == "shift":
                                shift_item(h + 1, s + 1)
                            else:
                                den_item(h - 1)
                    if s < HPH or more:
                        if r == 0 and u in (2, 4, 6):
                            split_qk(t + 1, 0, u // 2 - 1)
                        if r == 1:
                            if u == 0:
                                split_qk(t + 1, 0, 3)
                            if u in (2, 4, 6):
                                split_qk(t + 1, 1, u // 2 - 1)
                        if r == 2 and u == 0:
                            split_qk(t + 1, 1, 3)
                    if u == 3 and prev:
                        invert_sums(h - 1)

            for name, credit in (("ring_free", 2), ("sum0", 7), ("o_done", 1), ("qk_split", 2), ("xn_split", 2)):
                dve.sem_inc(s1[name], credit)
            for name, credit in (("sum2_free", 1), ("v_made", 1), ("v_split", 1), ("conv_free", 4)):
                dve.sem_inc(s2[name], credit)
            for c in range(NC):
                dve.wait_ge(s1[f"x_first{c}"], 16)
                moments(c)
            aggregate()
            dve.wait_ge(s_const, 48)
            stat_item(0, 0)
            stat_item(0, 1)
            for n, k in enumerate((1, 0, 2)):
                dve.wait_ge(s1[f"w_loaded{n % 2}"], 16 * (n // 2 + 1))
                hi, lo = (t_[:, k].rearrange("p c n -> p (c n)") for t_ in (w_hi, w_lo))
                src = stage[:, n % 2].rearrange("p c n -> p (c n)")
                dve.tensor_scalar(hi, src, WSCALE, None, ALU.mult).then_inc(s1["w_hi_done"], 1)
                dve.wait_ge(s1["w_hi_done"], n + 1)
                dve.scalar_tensor_tensor(out=lo, in0=src, scalar=WSCALE, in1=hi,
                                         op0=ALU.mult, op1=ALU.subtract).then_inc(s1["w_split"], 1)
                if n == 0:
                    for c in range(NC):
                        split_norm(0, 0, c, first=True)
                if n == 1:
                    split_qk(0, 0, 0)
            for n in range(1, 2 * NC):
                split_qk(0, n // NC, n % NC)
            for g in range(HPH):
                split_norm(0, 1, g, first=True)
                value_item(g, 0, g)
            for m in range(16):
                max_item(0, m)
            shift_item(0, 0)
            slot(0, 0, prev=False)
            with dve.Fori(0, B - 1) as i:
                ring.loop(i)
                step.loop(i)
                for s in range(1, HPI):
                    slot(i, s)
                slot(i + 1, 0)
            ring.done(B - 1)
            step.done(B - 1)
            for s in range(1, HPI):
                slot(B - 1, s, nxt=s < HPI - 1, more=False)
            add_tile(B * HPI - 1, HPI - 1, SEG - 1)
            den_item(B * HPI - 1)
            invert_sums(B * HPI - 1)

            step.per = 2 * STAT_STEPS
            mstep.per = 2 * MASK_STEPS

            def moments2(img, b, loads):
                dve.wait_ge(s2[f"x_in{b}"], 16 * loads)
                moments, aggregate, _, _ = statistics(dve, xo[b], step)
                for c in range(NC):
                    moments(c)
                aggregate()

            def group_sum(img, k):
                dve.wait_ge(s2["sum2_full"], (img - 1) * 2 + k + 1)
                (centre, finish)[k](qk_bank, s2["sum2_free"])

            def split_v(img, pos):
                dve.wait_ge(s2["v_cast"], 4 * img + pos + 1)
                dve.tensor_tensor(v_lo[:, pos], v32_v, v_hi[:, pos], ALU.subtract).then_inc(s2["v_split"], 1)

            def add_group(img, b, n):
                pos, co = n // NC, n % NC
                dve.wait_ge(s2["conv_full"], GROUPS * (img + 1) + n + 1)
                if pos == 0 and co == 0:
                    dve.wait_ge(s2["bias_in"], 4 * img + 4)
                dve.wait_ge(s2["conv_free"], IMG_READS * img + reads_to(pos - 1, co))
                for odd, factor in Y_OF[pos]:
                    y = xo_pair[b][:, co, :, odd]
                    dve.scalar_tensor_tensor(out=y, in0=bank[co][:], scalar=factor / WSCALE, in1=y,
                                             op0=ALU.mult, op1=ALU.add).then_inc(s2["conv_free"], 1)

            def image(img, b, loads=None):
                make_v(img, 3)
                add_group(img, b, 0)
                split_v(img, 3)
                for n in range(1, GROUPS):
                    add_group(img, b, n)
                    if loads is None:
                        continue
                    if n == 1:
                        moments2(img + 1, 1 - b, loads)
                    if n == 3:
                        group_sum(img + 1, 0)
                    if n == 4:
                        group_sum(img + 1, 1)
                    if n == 5:
                        for c in range(NC):
                            sums(img + 1, c)
                    if n == 6:
                        make_tables()
                    if 7 <= n < 9:
                        mask_chunk(img + 1, 2 * n - 14)
                        mask_chunk(img + 1, 2 * n - 13)
                    if n >= 11 and n < 14:
                        split_v(img + 1, n - 11)
                    if n >= 10 and n < 13:
                        make_v(img + 1, n - 10)

            dve.wait_ge(s1["sum1"], 7 + 7 * B * HPI)
            split_filters(0, 2, 2)
            split_v(0, 0)
            for ky in range(3):
                dve.wait_ge(s2[f"g12_loaded{ky % 2}"], 16 * (ky // 2 + 1))
                dve.tensor_tensor(g0[ky], g0[ky], g12[ky % 2], ALU.add).then_inc(s2["g_summed"], 1)
                if ky == 0:
                    make_v(0, 1)
                split_filters(1, ky, 3 + ky)
            split_v(0, 1)

            def less_column(ky):
                dve.wait_ge(s2[f"g12_loaded{ky % 2}"], 16 * (3, 2, 4)[ky])
                if ky > 0:
                    dve.wait_ge(s2["g_mixed"], ky)
                dve.tensor_tensor(filter_at(3, ky), g0[ky], g12[ky % 2], ALU.subtract).then_inc(s2["g_less"], 1)

            for n in range(GROUPS):
                add_group(0, 0, n)
                if 1 <= n < 4:
                    split_filters(3, n - 1, 4 + 2 * n)
                    split_filters(2, n - 1, 5 + 2 * n)
                if n < 3:
                    less_column(n)
                if n in (4, 6):
                    make_v(0, 2 + (n - 4) // 2)
                if n in (5, 7):
                    split_v(0, 2 + (n - 5) // 2)
                if n == 5:
                    moments2(1, 1, 1)
                if n in (FIRST_STATS, FIRST_STATS + 1):
                    group_sum(1, n - FIRST_STATS)
                if n == 10:
                    for c in range(NC):
                        sums(1, c)
                if n == 11:
                    make_tables()
                if n in (11, 12):
                    mask_chunk(1, 2 * n - 22)
                    mask_chunk(1, 2 * n - 21)
                if n >= 14:
                    split_v(1, n - 14)
                if n >= 13:
                    make_v(1, n - 13)
            split_v(1, 2)
            with dve.Fori(0, B // 2 - 1) as j:
                step.loop(j)
                mstep.loop(j)
                image(j * 2 + 1, 1, j + 1)
                image(j * 2 + 2, 0, j + 2)
            step.done(B // 2 - 1)
            mstep.done(B // 2 - 1)
            image(B - 1, 1)


_INS = ["x", "wqT", "wkT", "wvT", "chan", "bv", "wc", "const"]


def constants(np):
    c = np.zeros((P, C_END), np.float32)
    c[:, C_ID:C_ID + P] = np.eye(P)
    c[:, C_GRP:C_GRP + P] = np.kron(np.eye(P // GRP), np.full((GRP, GRP), 1.0 / GRP))
    c[:, C_ONE:C_ONE + D] = 1.0
    c[:, C_IOTA:C_IOTA + HW] = np.arange(1, HW + 1)
    c[:, C_POS:C_POS + HW] = np.linspace(-1.0, 1.0, HW)
    return c


def kernel(**inputs):
    import numpy as np
    import concourse.bacc as bacc
    from concourse.bass_utils import run_bass_kernel_spmd

    a = {k: np.asarray(v) for k, v in inputs.items()}
    column = [a[k].reshape(NC, P).T for k in
              ("L0_conv_bq", "L0_conv_bk", "L1_conv_bias", "L1_conv_mask_weight", "L1_conv_filter")]
    arrays = {
        "x": a["x"].reshape(B, C, S),
        "wqT": a["L0_conv_Wq"].T,
        "wkT": a["L0_conv_Wk"].T,
        "wvT": a["L0_conv_Wv"].T,
        "chan": np.concatenate(column, axis=1),
        "bv": a["L0_conv_bv"],
        "wc": a["L1_conv_weight"].transpose(2, 3, 1, 0).reshape(9, C, C),
        "const": constants(np),
    }
    arrays = {k: np.ascontiguousarray(v) for k, v in arrays.items()}
    nc = bacc.Bacc("TRN2", target_bir_lowering=False, num_devices=1)
    args = [nc.dram_tensor(k, arrays[k].shape, mybir.dt.from_np(arrays[k].dtype), kind="ExternalInput").ap()
            for k in _INS]
    out = nc.dram_tensor("out", (B, C, S), F32, kind="ExternalOutput").ap()
    build(nc, *args, out)
    r = run_bass_kernel_spmd(nc, [arrays], core_ids=[0])
    return r.results[0]["out"].reshape(B, C, HW, HW)
```
